# Optimizing a Trainium2 kernel written in Bass

```python
import numpy as np
import jax
import jax.numpy as jnp

def _softmax(x, axis=-1):
    return jax.nn.softmax(x, axis=axis)

def _gelu(x):
    return jax.nn.gelu(x, approximate=True)

def _silu(x):
    return jax.nn.silu(x)

def _sigmoid(x):
    return jax.nn.sigmoid(x)

def _layernorm(x, axis=-1, eps=1e-05):
    m = jnp.mean(x, axis=axis, keepdims=True)
    v = jnp.var(x, axis=axis, keepdims=True)
    return (x - m) / jnp.sqrt(v + eps)

def _scatter_add(tgt, idx, src, axis=0):
    return tgt.at[idx].add(src)

def _segment_sum(src, seg, n):
    return jax.ops.segment_sum(src, seg, n)
kernel_name = 'mk_sandwich_d1_jaxref_r8_f2dcad'

def setup_inputs(seed: int=0):
    np.random.seed(seed)
    _w = jnp.asarray

    def _L0_attn_setup():
        import jax, jax.numpy as jnp
        import numpy as np
        N_EMBD = 128
        N_HEAD = 16
        N_LAYER = 24
        LAYER_ID = 12
        B, T = (4, 512)
        Q = 64
        EPS = 1e-05 * 64

        def _static_params():
            C, H = (N_EMBD, N_HEAD)
            r01 = LAYER_ID / (N_LAYER - 1)
            r1a0 = 1.0 - LAYER_ID / N_LAYER
            ddd = np.arange(C, dtype=np.float64) / C
            maa_k = (1.0 - ddd ** r1a0).astype(np.float32).reshape(1, 1, C)
            maa_v = (1.0 - (ddd ** r1a0 + 0.3 * r01)).astype(np.float32).reshape(1, 1, C)
            maa_r = (1.0 - ddd ** (0.5 * r1a0)).astype(np.float32).reshape(1, 1, C)
            maa_g = maa_r.copy()
            h = np.arange(H, dtype=np.float64)
            decay = (-6.0 + 5.0 * (h / (H - 1)) ** (0.7 + 1.3 * r01)).astype(np.float32).reshape(H, 1)
            faaaa = (r01 * (1.0 - h / (H - 1))).astype(np.float32).reshape(H, 1)
            return (maa_k, maa_v, maa_r, maa_g, decay, faaaa)

        def _rwkv_forward(x, time_maa_k, time_maa_v, time_maa_r, time_maa_g, time_decay, time_faaaa, Wr, Wk, Wv, Wg, Wo, ln_w, ln_b):
            Bv, Tv, C = x.shape
            H = N_HEAD
            N = C // H
            nC = Tv // Q
            xx = jnp.pad(x, ((0, 0), (1, 0), (0, 0)))[:, :Tv] - x
            xk = x + xx * time_maa_k
            xv = x + xx * time_maa_v
            xr = x + xx * time_maa_r
            xg = x + xx * time_maa_g
            r = (xr @ Wr.T).reshape(Bv, Tv, H, N).transpose(0, 2, 1, 3)
            k = (xk @ Wk.T).reshape(Bv, Tv, H, N).transpose(0, 2, 3, 1)
            v = (xv @ Wv.T).reshape(Bv, Tv, H, N).transpose(0, 2, 1, 3)
            g = jax.nn.gelu(xg @ Wg.T, approximate=False)
            w = jnp.exp(-jnp.exp(time_decay))[:, 0]
            u = time_faaaa[:, 0]
            q = jnp.arange(Q)
            ws = (w ** Q).reshape(1, H, 1, 1)
            wk = (w[:, None] ** (Q - 1 - q)).reshape(1, H, 1, Q)
            wb = (w[:, None] ** q).reshape(1, H, Q, 1)
            i_idx = q[:, None]
            j_idx = q[None, :]
            e = jnp.maximum(i_idx - j_idx - 1, 0)
            Wmat = jnp.where(i_idx > j_idx, w[:, None, None] ** e, 0.0)
            Wmat = Wmat + jnp.eye(Q, dtype=x.dtype) * u[:, None, None]
            Wmat = Wmat.reshape(1, H, Q, Q)
            rr = r.reshape(Bv, H, nC, Q, N).transpose(2, 0, 1, 3, 4)
            kk = k.reshape(Bv, H, N, nC, Q).transpose(3, 0, 1, 2, 4)
            vv = v.reshape(Bv, H, nC, Q, N).transpose(2, 0, 1, 3, 4)

            def step(state, inp):
                rc, kc, vc = inp
                att = rc @ kc
                yc = att * Wmat @ vc + rc @ state * wb
                new_state = ws * state + kc * wk @ vc
                return (new_state, yc)
            state0 = jnp.zeros((Bv, H, N, N), dtype=x.dtype)
            _, ys = jax.lax.scan(step, state0, (rr, kk, vv))
            y = ys.transpose(1, 2, 0, 3, 4).reshape(Bv, H, Tv, N)
            y = y.transpose(0, 2, 1, 3)
            mean = y.mean(axis=-1, keepdims=True)
            var = y.var(axis=-1, keepdims=True)
            yn = (y - mean) / jnp.sqrt(var + EPS)
            yn = yn * ln_w.reshape(1, 1, H, N) + ln_b.reshape(1, 1, H, N)
            yn = yn.reshape(Bv, Tv, C)
            out = yn * g @ Wo.T
            return out
        key = jax.random.key(seed)
        ks = jax.random.split(key, 8)
        C = N_EMBD
        maa_k, maa_v, maa_r, maa_g, decay, faaaa = _static_params()
        std = 0.02
        return {'x': jax.random.normal(ks[0], (B, T, C), dtype=jnp.float32), 'time_maa_k': jnp.asarray(maa_k), 'time_maa_v': jnp.asarray(maa_v), 'time_maa_r': jnp.asarray(maa_r), 'time_maa_g': jnp.asarray(maa_g), 'time_decay': jnp.asarray(decay), 'time_faaaa': jnp.asarray(faaaa), 'Wr': jax.random.normal(ks[1], (C, C), dtype=jnp.float32) * std, 'Wk': jax.random.normal(ks[2], (C, C), dtype=jnp.float32) * std, 'Wv': jax.random.normal(ks[3], (C, C), dtype=jnp.float32) * std, 'Wg': jax.random.normal(ks[4], (C, C), dtype=jnp.float32) * std, 'Wo': jax.random.normal(ks[5], (C, C), dtype=jnp.float32) * std, 'ln_w': jnp.ones((C,), dtype=jnp.float32), 'ln_b': jnp.zeros((C,), dtype=jnp.float32)}
    _L0_attn_in = _L0_attn_setup()

    def _L0_ffn_setup():
        import jax, jax.numpy as jnp
        import numpy as np
        import math
        N_EMBD = 128
        HIDDEN = 4 * N_EMBD
        N_EXPERTS = 8
        TOP_K = 2
        B, T = (4, 256)

        def new_gelu(x):
            c = math.sqrt(2.0 / math.pi)
            return 0.5 * x * (1.0 + jnp.tanh(c * (x + 0.044715 * x * x * x)))

        def _moe_forward(x, Wfc_s, bfc_s, Wproj_s, bproj_s, Wr, Wfc, bfc, Wproj, bproj):
            Bb, Tt, C = x.shape
            xf = x.reshape(Bb * Tt, C)
            N = Bb * Tt
            shared = new_gelu(xf @ Wfc_s + bfc_s) @ Wproj_s + bproj_s
            logits = xf @ Wr
            probs = jax.nn.softmax(logits, axis=-1)
            topk_p, topk_i = jax.lax.top_k(probs, TOP_K)
            topk_p = topk_p / jnp.sum(topk_p, axis=-1, keepdims=True)
            gate = jnp.zeros((N, N_EXPERTS), dtype=xf.dtype)
            gate = gate.at[jnp.arange(N)[:, None], topk_i].add(topk_p)
            routed = jnp.zeros_like(xf)
            for e in range(N_EXPERTS):
                h = new_gelu(xf @ Wfc[e] + bfc[e]) @ Wproj[e] + bproj[e]
                routed = routed + h * gate[:, e:e + 1]
            return (shared + routed).reshape(Bb, Tt, C)
        key = jax.random.key(seed)
        ks = jax.random.split(key, 10)
        s = 0.02
        return {'x': jax.random.normal(ks[0], (B, T, N_EMBD), dtype=jnp.float32), 'Wfc_s': jax.random.normal(ks[1], (N_EMBD, HIDDEN), dtype=jnp.float32) * s, 'bfc_s': jnp.zeros((HIDDEN,), dtype=jnp.float32), 'Wproj_s': jax.random.normal(ks[2], (HIDDEN, N_EMBD), dtype=jnp.float32) * s, 'bproj_s': jnp.zeros((N_EMBD,), dtype=jnp.float32), 'Wr': jax.random.normal(ks[3], (N_EMBD, N_EXPERTS), dtype=jnp.float32) * s, 'Wfc': jax.random.normal(ks[4], (N_EXPERTS, N_EMBD, HIDDEN), dtype=jnp.float32) * s, 'bfc': jnp.zeros((N_EXPERTS, HIDDEN), dtype=jnp.float32), 'Wproj': jax.random.normal(ks[5], (N_EXPERTS, HIDDEN, N_EMBD), dtype=jnp.float32) * s, 'bproj': jnp.zeros((N_EXPERTS, N_EMBD), dtype=jnp.float32)}
    _L0_ffn_in = _L0_ffn_setup()
    _d = {'L0_attn_x': _L0_attn_in['x'], 'L0_attn_time_maa_k': _L0_attn_in['time_maa_k'], 'L0_attn_time_maa_v': _L0_attn_in['time_maa_v'], 'L0_attn_time_maa_r': _L0_attn_in['time_maa_r'], 'L0_attn_time_maa_g': _L0_attn_in['time_maa_g'], 'L0_attn_time_decay': _L0_attn_in['time_decay'], 'L0_attn_time_faaaa': _L0_attn_in['time_faaaa'], 'L0_attn_Wr': _L0_attn_in['Wr'], 'L0_attn_Wk': _L0_attn_in['Wk'], 'L0_attn_Wv': _L0_attn_in['Wv'], 'L0_attn_Wg': _L0_attn_in['Wg'], 'L0_attn_Wo': _L0_attn_in['Wo'], 'L0_attn_ln_w': _L0_attn_in['ln_w'], 'L0_attn_ln_b': _L0_attn_in['ln_b'], 'L0_ffn_Wfc_s': _L0_ffn_in['Wfc_s'], 'L0_ffn_bfc_s': _L0_ffn_in['bfc_s'], 'L0_ffn_Wproj_s': _L0_ffn_in['Wproj_s'], 'L0_ffn_bproj_s': _L0_ffn_in['bproj_s'], 'L0_ffn_Wr': _L0_ffn_in['Wr'], 'L0_ffn_Wfc': _L0_ffn_in['Wfc'], 'L0_ffn_bfc': _L0_ffn_in['bfc'], 'L0_ffn_Wproj': _L0_ffn_in['Wproj'], 'L0_ffn_bproj': _L0_ffn_in['bproj']}
    _x0 = _d['L0_attn_x']
    _d['L0_attn_x'] = jax.random.normal(jax.random.fold_in(jax.random.key(seed), 1), (8, 1024, 128), dtype=_x0.dtype)
    del _x0
    return _d

def reference(L0_attn_x, L0_attn_time_maa_k, L0_attn_time_maa_v, L0_attn_time_maa_r, L0_attn_time_maa_g, L0_attn_time_decay, L0_attn_time_faaaa, L0_attn_Wr, L0_attn_Wk, L0_attn_Wv, L0_attn_Wg, L0_attn_Wo, L0_attn_ln_w, L0_attn_ln_b, L0_ffn_Wfc_s, L0_ffn_bfc_s, L0_ffn_Wproj_s, L0_ffn_bproj_s, L0_ffn_Wr, L0_ffn_Wfc, L0_ffn_bfc, L0_ffn_Wproj, L0_ffn_bproj):

    def _L0_attn_ref(x, time_maa_k, time_maa_v, time_maa_r, time_maa_g, time_decay, time_faaaa, Wr, Wk, Wv, Wg, Wo, ln_w, ln_b):
        import jax, jax.numpy as jnp
        import numpy as np
        N_EMBD = 128
        N_HEAD = 16
        N_LAYER = 24
        LAYER_ID = 12
        B, T = (4, 512)
        Q = 64
        EPS = 1e-05 * 64

        def _static_params():
            C, H = (N_EMBD, N_HEAD)
            r01 = LAYER_ID / (N_LAYER - 1)
            r1a0 = 1.0 - LAYER_ID / N_LAYER
            ddd = np.arange(C, dtype=np.float64) / C
            maa_k = (1.0 - ddd ** r1a0).astype(np.float32).reshape(1, 1, C)
            maa_v = (1.0 - (ddd ** r1a0 + 0.3 * r01)).astype(np.float32).reshape(1, 1, C)
            maa_r = (1.0 - ddd ** (0.5 * r1a0)).astype(np.float32).reshape(1, 1, C)
            maa_g = maa_r.copy()
            h = np.arange(H, dtype=np.float64)
            decay = (-6.0 + 5.0 * (h / (H - 1)) ** (0.7 + 1.3 * r01)).astype(np.float32).reshape(H, 1)
            faaaa = (r01 * (1.0 - h / (H - 1))).astype(np.float32).reshape(H, 1)
            return (maa_k, maa_v, maa_r, maa_g, decay, faaaa)

        def _rwkv_forward(x, time_maa_k, time_maa_v, time_maa_r, time_maa_g, time_decay, time_faaaa, Wr, Wk, Wv, Wg, Wo, ln_w, ln_b):
            Bv, Tv, C = x.shape
            H = N_HEAD
            N = C // H
            nC = Tv // Q
            xx = jnp.pad(x, ((0, 0), (1, 0), (0, 0)))[:, :Tv] - x
            xk = x + xx * time_maa_k
            xv = x + xx * time_maa_v
            xr = x + xx * time_maa_r
            xg = x + xx * time_maa_g
            r = (xr @ Wr.T).reshape(Bv, Tv, H, N).transpose(0, 2, 1, 3)
            k = (xk @ Wk.T).reshape(Bv, Tv, H, N).transpose(0, 2, 3, 1)
            v = (xv @ Wv.T).reshape(Bv, Tv, H, N).transpose(0, 2, 1, 3)
            g = jax.nn.gelu(xg @ Wg.T, approximate=False)
            w = jnp.exp(-jnp.exp(time_decay))[:, 0]
            u = time_faaaa[:, 0]
            q = jnp.arange(Q)
            ws = (w ** Q).reshape(1, H, 1, 1)
            wk = (w[:, None] ** (Q - 1 - q)).reshape(1, H, 1, Q)
            wb = (w[:, None] ** q).reshape(1, H, Q, 1)
            i_idx = q[:, None]
            j_idx = q[None, :]
            e = jnp.maximum(i_idx - j_idx - 1, 0)
            Wmat = jnp.where(i_idx > j_idx, w[:, None, None] ** e, 0.0)
            Wmat = Wmat + jnp.eye(Q, dtype=x.dtype) * u[:, None, None]
            Wmat = Wmat.reshape(1, H, Q, Q)
            rr = r.reshape(Bv, H, nC, Q, N).transpose(2, 0, 1, 3, 4)
            kk = k.reshape(Bv, H, N, nC, Q).transpose(3, 0, 1, 2, 4)
            vv = v.reshape(Bv, H, nC, Q, N).transpose(2, 0, 1, 3, 4)

            def step(state, inp):
                rc, kc, vc = inp
                att = rc @ kc
                yc = att * Wmat @ vc + rc @ state * wb
                new_state = ws * state + kc * wk @ vc
                return (new_state, yc)
            state0 = jnp.zeros((Bv, H, N, N), dtype=x.dtype)
            _, ys = jax.lax.scan(step, state0, (rr, kk, vv))
            y = ys.transpose(1, 2, 0, 3, 4).reshape(Bv, H, Tv, N)
            y = y.transpose(0, 2, 1, 3)
            mean = y.mean(axis=-1, keepdims=True)
            var = y.var(axis=-1, keepdims=True)
            yn = (y - mean) / jnp.sqrt(var + EPS)
            yn = yn * ln_w.reshape(1, 1, H, N) + ln_b.reshape(1, 1, H, N)
            yn = yn.reshape(Bv, Tv, C)
            out = yn * g @ Wo.T
            return out
        return _rwkv_forward(x, time_maa_k, time_maa_v, time_maa_r, time_maa_g, time_decay, time_faaaa, Wr, Wk, Wv, Wg, Wo, ln_w, ln_b)

    def _L0_ffn_ref(x, Wfc_s, bfc_s, Wproj_s, bproj_s, Wr, Wfc, bfc, Wproj, bproj):
        import jax, jax.numpy as jnp
        import numpy as np
        import math
        N_EMBD = 128
        HIDDEN = 4 * N_EMBD
        N_EXPERTS = 8
        TOP_K = 2
        B, T = (4, 256)

        def new_gelu(x):
            c = math.sqrt(2.0 / math.pi)
            return 0.5 * x * (1.0 + jnp.tanh(c * (x + 0.044715 * x * x * x)))

        def _moe_forward(x, Wfc_s, bfc_s, Wproj_s, bproj_s, Wr, Wfc, bfc, Wproj, bproj):
            Bb, Tt, C = x.shape
            xf = x.reshape(Bb * Tt, C)
            N = Bb * Tt
            shared = new_gelu(xf @ Wfc_s + bfc_s) @ Wproj_s + bproj_s
            logits = xf @ Wr
            probs = jax.nn.softmax(logits, axis=-1)
            topk_p, topk_i = jax.lax.top_k(probs, TOP_K)
            topk_p = topk_p / jnp.sum(topk_p, axis=-1, keepdims=True)
            gate = jnp.zeros((N, N_EXPERTS), dtype=xf.dtype)
            gate = gate.at[jnp.arange(N)[:, None], topk_i].add(topk_p)
            routed = jnp.zeros_like(xf)
            for e in range(N_EXPERTS):
                h = new_gelu(xf @ Wfc[e] + bfc[e]) @ Wproj[e] + bproj[e]
                routed = routed + h * gate[:, e:e + 1]
            return (shared + routed).reshape(Bb, Tt, C)
        return _moe_forward(x, Wfc_s, bfc_s, Wproj_s, bproj_s, Wr, Wfc, bfc, Wproj, bproj)
    x = L0_attn_x
    x = x + _layernorm(_L0_attn_ref(_layernorm(x, axis=-1), L0_attn_time_maa_k, L0_attn_time_maa_v, L0_attn_time_maa_r, L0_attn_time_maa_g, L0_attn_time_decay, L0_attn_time_faaaa, L0_attn_Wr, L0_attn_Wk, L0_attn_Wv, L0_attn_Wg, L0_attn_Wo, L0_attn_ln_w, L0_attn_ln_b), axis=-1)
    x = x + _layernorm(_L0_ffn_ref(_layernorm(x, axis=-1), L0_ffn_Wfc_s, L0_ffn_bfc_s, L0_ffn_Wproj_s, L0_ffn_bproj_s, L0_ffn_Wr, L0_ffn_Wfc, L0_ffn_bfc, L0_ffn_Wproj, L0_ffn_bproj), axis=-1)
    return x

_drawn_inputs = setup_inputs


def setup_inputs(seed=0):
    import zlib

    import numpy as np

    out = dict(_drawn_inputs(seed))
    spreads = {'L0_attn_ln_w': (1.0, 0.2),
     'L0_attn_ln_b': (0.0, 0.1),
     'L0_ffn_bfc_s': (0.0, 0.1),
     'L0_ffn_bproj_s': (0.0, 0.1),
     'L0_ffn_bfc': (0.0, 0.1),
     'L0_ffn_bproj': (0.0, 0.1)}
    factors = {}
    for name, (base, spread) in spreads.items():
        noise = np.random.default_rng([zlib.crc32(name.encode()), seed]).standard_normal(out[name].shape)
        drawn = base * np.exp(spread * noise) if base else spread * noise
        out[name] = jnp.asarray(drawn.astype(out[name].dtype))
    for name, factor in factors.items():
        out[name] = (out[name] * factor).astype(out[name].dtype)
    return out
```

```python
import concourse.bass as bass
from concourse import mybir
from contextlib import ExitStack

F32 = mybir.dt.float32
F16 = mybir.dt.float16
U32 = mybir.dt.uint32
ALU = mybir.AluOpType
ACT = mybir.ActivationFunctionType
AX = mybir.AxisListType

B, T, C = 8, 1024, 128
H, N = 16, 8
P = 128
TOK = 512
Q = TOK // P
TILES = B * T // TOK
PAIRS = TILES // 2
E = 8
EXP = E + 1
HID = 512
J = HID // P
EPS_LN = 1e-5
EPS_GN = 1e-5 * 64
W_SCALE = 2.0 ** 8
X_SCALE = 2.0 ** 8
H_SCALE = 2.0 ** 6
FC_DESCALE = 1.0 / (W_SCALE * X_SCALE)
PROJ_DESCALE = 1.0 / (H_SCALE * W_SCALE)
NEWTON = 3
GUESS = 0x5F3759DF
R_, K_, V_, G_, O_ = range(5)
NB_BFC = EXP * J
NB = NB_BFC + 6
MAA_K, MAA_V, MAA_R, MAA_G, LN_W, LN_B = range(NB_BFC, NB)
RS = 4
CH = 512


def is_int(t):
    return isinstance(t, int)


def build(nc, x, maa_k, maa_v, maa_r, maa_g, decay, faaaa, wr, wk, wv, wg, wo, ln_w, ln_b,
          wfc_s, bfc_s, wproj_s, bproj_s, w_router, wfc, bfc, wproj, bproj, out):
    ctx = ExitStack()
    with ctx:
        def sb(name, shape, dt=F32):
            return ctx.enter_context(nc.sbuf_tensor(name, shape, dt))

        def sem(name):
            return ctx.enter_context(nc.semaphore(name))

        xres = sb("xres", [P, TILES * TOK])
        yres = sb("yres", [P, TILES * TOK])
        gres = sb("gres", [P, TILES * TOK])
        wexp = sb("wexp", [P, (2 * EXP + 1) * CH])
        wt = sb("wt", [P, 5, C])
        wvrep = sb("wvrep", [P, N, P])
        ident = sb("ident", [P, P])
        sel = sb("sel", [P, 32])
        selT = sb("selT", [H, P])
        pcol = sb("pcol", [P, NB])
        wcol = sb("wcol", [P, 1])
        ucol = sb("ucol", [P, 1])
        neghalf = sb("neghalf", [P, Q])
        iota8 = sb("iota8", [P, E])
        wrt = sb("wrt", [P, E])
        wrt_hi = sb("wrt_hi", [P, E], F16)
        wrt_lo = sb("wrt_lo", [P, E], F16)
        bprow = sb("bprow", [EXP, C])
        bps = sb("bps", [EXP, C])
        dcol = sb("dcol", [H, 2])
        gates = [sb(f"gates{i}", [P, Q, EXP]) for i in range(2)]

        WORK = 16400
        work = sb("work", [P, WORK])
        cut_at = [0]

        def cut(n, dt=F32):
            words = n if dt == F32 else n // 2
            a = cut_at[0]
            cut_at[0] += words
            assert cut_at[0] <= WORK, cut_at
            v = work[:, a:a + words]
            return v if dt == F32 else v.bitcast(dt)

        xn = cut(TOK)
        xT = [cut(TOK + 1) for _ in range(2)]
        cut_at[0] += cut_at[0] % 2
        xx = cut(TOK)
        xmix_v = [cut(TOK) for _ in range(2)]
        xmix_k, xmix_r, xmix_g = (cut(TOK) for _ in range(3))
        kch = [cut(TOK) for _ in range(2)]
        rch = [cut(TOK) for _ in range(2)]
        kv = [cut(TOK) for _ in range(2)]
        S_AT = cut_at[0]
        wraw = [cut(C) for _ in range(5)]
        prow = cut(C)[0:NB, :]
        dexp = cut(2)
        cut_at[0] = S_AT
        S = [cut(TOK + 2) for _ in range(N)]
        rS = [cut(TOK) for _ in range(RS)]
        uk = cut(TOK)
        ruk = cut(TOK)
        ych = [cut(TOK) for _ in range(2)]
        rk = cut(Q * H)
        ast = cut(Q * 6)
        amv = [cut(Q * 2) for _ in range(2)]
        ave = cut(Q)
        ars = [cut(Q) for _ in range(2)]
        A_END = cut_at[0]
        cut_at[0] = 0
        s64 = cut(Q * H)
        v64 = cut(Q * H)
        gve = cut(Q * H)
        ghv = cut(Q * H)
        gshift = cut(Q * H).bitcast(U32)
        grs = cut(Q * H)
        gsq = cut(Q * H)
        gtm = cut(Q * H)
        gtf = cut(Q * H)
        yc = cut(TOK)
        sq = cut(TOK)
        yn = [cut(TOK) for _ in range(2)]
        zT = cut(TOK)
        zz = cut(TOK)
        dd = cut(TOK)
        xn2 = cut(TOK)
        xh = [cut(TOK, F16) for _ in range(2)]
        xl = [cut(TOK, F16) for _ in range(2)]
        h32 = [cut(TOK) for _ in range(J)]
        hh = [[cut(TOK, F16) for _ in range(J)] for _ in range(2)]
        hl = [[cut(TOK, F16) for _ in range(J)] for _ in range(2)]
        acc = [cut(TOK) for _ in range(2)]
        dd2 = cut(TOK)
        ob = cut(TOK)
        g9 = cut(TOK)[0:EXP, :]
        ost = cut(Q * 6)
        omv = cut(Q * 2)
        ove = cut(Q)
        ors = cut(Q)
        xst = cut(Q * 6)
        xmv = cut(Q * 2)
        xve = cut(Q)
        xrs = cut(Q)
        fst = cut(Q * 6)
        fmv = cut(Q * 2)
        fve = cut(Q)
        frs = cut(Q)
        mx = cut(Q)
        lg = cut(Q * E)
        ex = cut(Q * E)
        se = cut(Q)
        rse = cut(Q)
        pr = cut(Q * E)
        top = cut(Q * 8)
        tix = cut(Q * 8).bitcast(U32)
        tif = cut(Q * 8)
        s2 = cut(Q)
        r2 = cut(Q)
        g2 = cut(Q * 2)
        eq = [cut(Q * E) for _ in range(2)]

        bank = [ctx.enter_context(nc.psum_tensor(f"bank{i}", [P, 512], F32)) for i in range(8)]

        s = {n: sem(n) for n in (
            "params_in wexp_in x_first_in x_second_in x_rest_in out_done "
            "const pool_set setup_t setup_ev decay_ps decay_e decay_r wvrep_done xt0_zero split_s split_hi split_lo "
            "a_stats a_mv a_ve a_rstd a_xn a_xT_ps a_xT a_edge a_xx a_mix a_k_ps a_r_ps a_g_ps a_k a_uk a_r a_g "
            "a_vrep a_kv a_carry a_scan a_rs a_sel a_yev a_vt a_ruk a_rk_ps a_rk a_yu a_yT a_y "
            "g_s g_yc g_sq g_v g_ve g_hv g_shift g_guess g_newton g_yn b_ynT b_zT b_zz b_o b_ost b_omv b_ove b_ors b_dd b_x1 "
            "b_xst b_xmv b_xve b_xrs b_xn2 b_xn2T b_xh b_xl b_lg b_mx b_lgd b_ex b_se b_rse b_pr b_top b_tix "
            "b_s2 b_r2 b_g2 b_eq b_gate b_gT b_g9 b_bias b_acc "
            "b_fc b_gelu b_hi b_lo b_proj b_comb f_st f_mv f_ve f_rs f_dd f_ob").split()}

        bkA, bkB, bkC, bkD = bank[0:4]
        bkV, bkY = bank[4:6], bank[6:8]
        bkF, bkP, bkX, bkZ = bank[0:4], bank[4:6], bank[6], bank[7]

        def tile_of(res, t):
            return res[:, bass.ts(t, TOK)]

        def chunk_of(res, t, q):
            return res[:, bass.ds(t * TOK + q * P, P)]

        def w_hi(i):
            return wexp[:, i * CH:i * CH + CH // 2].bitcast(F16)

        def w_lo(i):
            return wexp[:, i * CH + CH // 2:(i + 1) * CH].bitcast(F16)

        def w_stage(i):
            return wexp[:, (i + 1) * CH:(i + 2) * CH]

        def wait_past(eng, name, value):
            if not isinstance(value, int) or value > 0:
                eng.wait_ge(s[name], value)

        def wait_apart(eng, name, value):
            if not isinstance(value, int):
                eng.to_reg(value)
            eng.wait_ge(s["const"], 1)
            eng.wait_ge(s[name], value)

        block = ctx.enter_context(nc.Block())

        @block.sync
        def _(sp):
            for i, w in enumerate((wr, wk, wv, wg, wo)):
                sp.dma_start(wraw[i], w).then_inc(s["params_in"], 16)
            sp.dma_start(prow[0:E * J, :], bfc.rearrange("e (j p) -> (e j) p", p=P)).then_inc(s["params_in"], 16)
            sp.dma_start(prow[E * J:NB_BFC, :], bfc_s.rearrange("(j p) -> j p", p=P)).then_inc(s["params_in"], 16)
            for r, m in ((MAA_K, maa_k), (MAA_V, maa_v), (MAA_R, maa_r), (MAA_G, maa_g)):
                sp.dma_start(prow[r:r + 1, :], m.rearrange("a b c -> (a b) c")).then_inc(s["params_in"], 16)
            for r, m in ((LN_W, ln_w), (LN_B, ln_b)):
                sp.dma_start(prow[r:r + 1, :], m.rearrange("(a c) -> a c", a=1)).then_inc(s["params_in"], 16)
            sp.dma_start(dcol[:, 0:1], decay).then_inc(s["params_in"], 16)
            sp.dma_start(dcol[:, 1:2], faaaa).then_inc(s["params_in"], 16)
            sp.dma_start(wrt[:, :], w_router).then_inc(s["params_in"], 16)
            sp.dma_start(bprow[0:E, :], bproj).then_inc(s["params_in"], 16)
            sp.dma_start(bprow[E:EXP, :], bproj_s.rearrange("(a c) -> a c", a=1)).then_inc(s["params_in"], 16)
            xv = x.rearrange("b (k p) c -> p b k c", p=P)
            xd = xres[:, :].rearrange("p (b k c) -> p b k c", b=B, c=C)
            sp.dma_start(xd[:, 0, :, :], xv[:, 0, :, :]).then_inc(s["x_first_in"], 16)
            for b in range(1, B):
                sp.dma_start(xd[:, b, :, :], xv[:, b, :, :]).then_inc(s["x_second_in" if b == 1 else "x_rest_in"], 16)
            for e in range(EXP):
                sp.dma_start(w_stage(e), wfc[e] if e < E else wfc_s).then_inc(s["wexp_in"], 16)
            for e in range(EXP):
                src = wproj[e] if e < E else wproj_s
                sp.dma_start(w_stage(EXP + e).rearrange("p (j c) -> p j c", c=C),
                             src.rearrange("(j p) c -> p j c", p=P)).then_inc(s["wexp_in"], 16)

            with sp.Fori(0, PAIRS) as i:
                for half in range(2):
                    sp.wait_ge(s["f_ob"], 2 * i + half + 1)
                    sp.dma_start(out[bass.ds(i, 1), half * TOK:(half + 1) * TOK, :]
                                 .rearrange("b (k p) c -> p (b k) c", p=P),
                                 ob.rearrange("p (k c) -> p k c", c=C)).then_inc(s["out_done"], 16)
            sp.wait_ge(s["out_done"], 16 * TILES)

        N_PARAMS = 16 * (5 + 2 + 4 + 2 + 3 + 2)

        @block.gpsimd
        def _(pool):
            pool.memset(ident[:, :], 0.0).then_inc(s["pool_set"], 1)
            pool.memset(sel[:, :], 1.0).then_inc(s["pool_set"], 1)
            pool.memset(selT[:, :], 1.0).then_inc(s["pool_set"], 1)
            pool.memset(neghalf[:, :], -0.5).then_inc(s["const"], 1)
            pool.iota(iota8[:, :], pattern=[[1, E]], base=0, channel_multiplier=0,
                      allow_small_or_imprecise_dtypes=True).then_inc(s["const"], 1)
            for i in range(2):
                pool.memset(gates[i][:, :, E:EXP], PROJ_DESCALE).then_inc(s["const"], 1)
            pool.wait_ge(s["pool_set"], 3)
            pool.affine_select(out=ident[:, :], in_=ident[:, :], compare_op=ALU.not_equal, fill=1.0,
                               base=0, pattern=[[-1, P]], channel_multiplier=1).then_inc(s["const"], 1)
            pool.affine_select(out=sel[:, :], in_=sel[:, :], compare_op=ALU.is_ge, fill=0.0,
                               base=0, pattern=[[-N, 32]], channel_multiplier=1).then_inc(s["pool_set"], 1)
            pool.affine_select(out=selT[:, :], in_=selT[:, :], compare_op=ALU.is_ge, fill=0.0,
                               base=0, pattern=[[1, P]], channel_multiplier=-N).then_inc(s["pool_set"], 1)
            pool.wait_ge(s["pool_set"], 5)
            pool.affine_select(out=sel[:, :], in_=sel[:, :], compare_op=ALU.is_ge, fill=0.0,
                               base=N - 1, pattern=[[N, 32]], channel_multiplier=-1).then_inc(s["const"], 1)
            pool.affine_select(out=selT[:, :], in_=selT[:, :], compare_op=ALU.is_ge, fill=0.0,
                               base=N - 1, pattern=[[-1, P]], channel_multiplier=N).then_inc(s["const"], 1)

            def rsqrt(var, ve, rs, eps, s_in, n_in, s_ve, s_rs, t):
                wait_apart(pool, s_in, n_in)
                pool.tensor_scalar(ve, var, 1.0, eps, ALU.mult, ALU.add).then_inc(s[s_ve], 1)
                pool.wait_ge(s[s_ve], t + 1)
                pool.tensor_tensor(rs, ve, neghalf[:, :], ALU.pow).then_inc(s[s_rs], 1)

            def variance(mv):
                return mv.rearrange("p (q two) -> p q two", two=2)[:, :, 1]

            def a_rstd(t, par):
                rsqrt(variance(amv[par]), ave, ars[par], EPS_LN, "a_mv", Q * t + Q, "a_ve", "a_rstd", t)

            def a_shift(t, par, pair):
                pool.wait_ge(s["a_xT"], t + 1)
                if par:
                    pool.wait_ge(s["a_edge"], pair + 1)
                pool.tensor_tensor(xx, xT[par][:, 0:TOK], xT[par][:, 1:TOK + 1], ALU.subtract).then_inc(s["a_xx"], 1)

            def a_rs(t, par, m):
                n = N * t + m
                pool.wait_ge(s["a_sel"], n + 1)
                if m == 0:
                    pool.wait_ge(s["a_r"], t + 1)
                pool.wait_ge(s["a_scan"], n + 1)
                pool.tensor_tensor(rS[m % RS], S[m][:, 0:TOK], rch[par], ALU.mult).then_inc(s["a_rs"], 1)

            def a_ruk(t, par):
                wait_past(pool, "a_rk_ps", t)
                pool.wait_ge(s["a_r"], t + 1)
                pool.wait_ge(s["a_uk"], t + 1)
                pool.tensor_tensor(ruk, uk, rch[par], ALU.mult).then_inc(s["a_ruk"], 1)

            def a_tile(pair, par):
                t = 2 * pair + par
                for m in range(N):
                    a_rs(t, par, m)
                    if m == 1:
                        a_ruk(t, par)
                    if m == 2 and not (is_int(t) and t + 1 >= TILES):
                        a_shift(t + 1, 1 - par, pair)
                    if m == 6 and not (is_int(t) and t + 2 >= TILES):
                        a_rstd(t + 2, par)

            pool.wait_ge(s["const"], 7)
            a_rstd(0, 0)
            pool.wait_ge(s["xt0_zero"], 1)
            a_rstd(1, 1)
            a_shift(0, 0, 0)
            a_tile(0, 0)
            a_tile(0, 1)
            with pool.Fori(1, PAIRS - 1) as i:
                a_tile(i, 0)
                a_tile(i, 1)
            a_tile(PAIRS - 1, 0)
            a_tile(PAIRS - 1, 1)

            def g_piece(u, e, up):
                if e == 2:
                    wait_apart(pool, "g_v", u + 1)
                    pool.tensor_scalar(gve, v64, 1.0 / N, EPS_GN, ALU.mult, ALU.add).then_inc(s["g_ve"], 1)
                    wait_apart(pool, "g_ve", u + 1)
                    pool.tensor_scalar(ghv, gve, -0.5, 0.0, ALU.mult, ALU.add).then_inc(s["g_hv"], 1)
                if 3 <= e < 3 + NEWTON:
                    n = 4 * NEWTON * u + 4 * (e - 3)
                    if e == 3:
                        pool.wait_ge(s["g_guess"], u + 1)
                        pool.wait_ge(s["g_hv"], u + 1)
                    else:
                        pool.wait_ge(s["g_newton"], n)
                    pool.tensor_tensor(gsq, grs, grs, ALU.mult).then_inc(s["g_newton"], 1)
                    pool.wait_ge(s["g_newton"], n + 1)
                    pool.tensor_tensor(gtm, gsq, ghv, ALU.mult).then_inc(s["g_newton"], 1)
                    wait_apart(pool, "g_newton", n + 2)
                    pool.tensor_scalar(gtf, gtm, 1.0, 1.5, ALU.mult, ALU.add).then_inc(s["g_newton"], 1)
                    pool.wait_ge(s["g_newton"], n + 3)
                    pool.tensor_tensor(grs, grs, gtf, ALU.mult).then_inc(s["g_newton"], 1)
                if e == 3 + NEWTON:
                    wait_past(pool, "b_ynT", u - 1)
                    pool.wait_ge(s["g_newton"], 4 * NEWTON * (u + 1))
                    pool.tensor_tensor(yn[up].rearrange("p (h m) -> p h m", m=N),
                                       yc.rearrange("p (h m) -> p h m", m=N),
                                       grs.unsqueeze(2).to_broadcast([P, Q * H, N]), ALU.mult).then_inc(s["g_yn"], 1)

            def b_gate(u):
                pool.wait_ge(s["b_zT"], u + 1)
                pool.tensor_tensor(zz, zT, tile_of(gres, u), ALU.mult).then_inc(s["b_zz"], 1)

            def b_ors(u):
                rsqrt(variance(omv), ove, ors, EPS_LN, "b_omv", Q * u + Q, "b_ove", "b_ors", u)

            def b_x1(u):
                pool.wait_ge(s["b_dd"], Q * u + Q)
                pool.tensor_tensor(tile_of(xres, u), tile_of(xres, u), dd, ALU.add).then_inc(s["b_x1"], 1)

            def b_xrs(u):
                rsqrt(variance(xmv), xve, xrs, EPS_LN, "b_xmv", Q * u + Q, "b_xve", "b_xrs", u)

            def f_rs(t):
                rsqrt(variance(fmv), fve, frs, EPS_LN, "f_mv", Q * t + Q, "f_ve", "f_rs", t)

            def f_out(t):
                pool.wait_ge(s["f_dd"], Q * t + Q)
                wait_past(pool, "out_done", 16 * t)
                pool.tensor_tensor(ob, tile_of(xres, t), dd2, ALU.add).then_inc(s["f_ob"], 1)

            def b_hi(t, g, j, par):
                n = J * g + j
                if j == 0:
                    pool.wait_ge(s["b_proj"], g + 1)
                wait_apart(pool, "b_gelu", n + 1)
                pool.tensor_scalar(hh[par][j], h32[j], H_SCALE, 0.0, ALU.mult, ALU.add).then_inc(s["b_hi"], 1)

            def b_piece(u, e):
                if e == 2:
                    b_gate(u)
                if e == 3:
                    b_ors(u)
                if e == 4:
                    b_x1(u)
                if e == 5:
                    b_xrs(u)

            def f_piece(t, e):
                if e == 1:
                    f_rs(t)
                if e == 2:
                    f_out(t)

            def b_tile(t, tp):
                for e in range(EXP):
                    for j in range(J):
                        b_hi(t, EXP * t + e, j, (EXP * tp + e) % 2)
                    if not is_int(t) or t > 0:
                        f_piece(t - 1, e)
                    if not is_int(t) or t + 1 < TILES:
                        b_piece(t + 1, e)
                    if not is_int(t) or t + 2 < TILES:
                        g_piece(t + 2, e, tp)

            for u in range(2):
                for e in range(EXP):
                    g_piece(u, e, u)
            for e in range(EXP):
                b_piece(0, e)
            b_tile(0, 0)
            b_tile(1, 1)
            with pool.Fori(1, PAIRS - 1) as i:
                b_tile(2 * i, 0)
                b_tile(2 * i + 1, 1)
            b_tile(TILES - 2, 0)
            b_tile(TILES - 1, 1)
            for e in range(EXP):
                f_piece(TILES - 1, e)

        @block.scalar
        def _(act):
            def copy(o, i):
                return act.activation(o, i, ACT.Copy)

            act.wait_ge(s["decay_ps"], 1)
            act.activation(dexp[:, 0:1], bkV[0][:, 0:1], ACT.Exp).then_inc(s["decay_e"], 1)
            copy(ucol[:, :], bkV[0][:, 1:2]).then_inc(s["decay_r"], 1)
            act.wait_ge(s["decay_e"], 1)
            act.activation(wcol[:, :], dexp[:, 0:1], ACT.Exp, scale=-1.0).then_inc(s["decay_r"], 1)
            for n in range(5):
                act.wait_ge(s["setup_t"], n + 1)
                copy(wt[:, n, :], bank[n % 4][:, 0:C]).then_inc(s["setup_ev"], 1)
            act.wait_ge(s["setup_t"], 6)
            copy(pcol[:, :], bkV[1][:, 0:NB]).then_inc(s["setup_ev"], 1)
            act.activation(bps[:, :], bprow[:, :], ACT.Copy, scale=1.0 / PROJ_DESCALE).then_inc(s["setup_ev"], 1)
            act.activation(wrt_hi[:, :], wrt[:, :], ACT.Copy, scale=W_SCALE).then_inc(s["setup_ev"], 1)

            def a_xT(t, par):
                act.wait_ge(s["a_xT_ps"], t + 1)
                copy(xT[par][:, 1:TOK + 1], bkA[:, :]).then_inc(s["a_xT"], 1)
                if par:
                    wait_past(act, "a_xT", t)
                    copy(xT[1][:, 0:1], xT[0][:, TOK:TOK + 1]).then_inc(s["a_edge"], 1)

            def a_kr(t, par):
                act.wait_ge(s["a_k_ps"], t + 1)
                copy(kch[par], bkC[:, :]).then_inc(s["a_k"], 1)
                wait_past(act, "a_ruk", t)
                act.activation(uk, bkC[:, :], ACT.Copy, scale=ucol[:, 0:1]).then_inc(s["a_uk"], 1)
                act.wait_ge(s["a_r_ps"], t + 1)
                copy(rch[par], bkB[:, :]).then_inc(s["a_r"], 1)

            def a_g(t):
                act.wait_ge(s["a_g_ps"], t + 1)
                act.activation(tile_of(gres, t), bkD[:, :], ACT.Gelu).then_inc(s["a_g"], 1)

            def a_rk(t):
                act.wait_ge(s["a_rk_ps"], t + 1)
                wait_past(act, "a_yu", t)
                copy(rk, bkB[:, 0:Q * H]).then_inc(s["a_rk"], 1)

            def a_yev(t, b):
                act.wait_ge(s["a_sel"], N * t + N // 2 * (b + 1) + RS)
                copy(ych[b], bkY[b][:, :]).then_inc(s["a_yev"], 1)

            def a_tile(t, par, last):
                if not last:
                    a_xT(t + 1, 1 - par)
                a_rk(t)
                a_yev(t, 0)
                if not last:
                    a_kr(t + 1, 1 - par)
                    a_g(t + 1)
                a_yev(t, 1)

            act.wait_ge(s["setup_ev"], 8)
            a_xT(0, 0)
            a_kr(0, 0)
            a_g(0)
            a_tile(0, 0, False)
            a_tile(1, 1, False)
            with act.Fori(1, PAIRS - 1) as i:
                a_tile(2 * i, 0, False)
                a_tile(2 * i + 1, 1, False)
            a_tile(TILES - 2, 0, False)
            a_tile(TILES - 1, 1, True)

            act.wait_ge(s["wexp_in"], 16 * 2 * EXP)
            for i in range(2 * EXP):
                if i:
                    act.wait_ge(s["split_lo"], i)
                act.activation(w_hi(i), w_stage(i), ACT.Copy, scale=W_SCALE).then_inc(s["split_hi"], 1)

            def g_piece(u, e):
                if e == 1:
                    act.wait_ge(s["g_yc"], u + 1)
                    act.activation(sq, yc, ACT.Square).then_inc(s["g_sq"], 1)

            def b_piece(u, e, up):
                if e == 1:
                    act.wait_ge(s["b_ynT"], u + 1)
                    act.activation(zT, bkX[:, :], ACT.Identity, bias=pcol[:, LN_B:LN_B + 1],
                                   scale=pcol[:, LN_W:LN_W + 1]).then_inc(s["b_zT"], 1)
                if e == 6:
                    act.wait_ge(s["b_xn2T"], u + 1)
                    act.activation(xh[up], bkX[:, :], ACT.Copy, scale=X_SCALE).then_inc(s["b_xh"], 1)
                if e == 8:
                    act.wait_ge(s["b_lgd"], u + 1)
                    act.activation(ex, lg, ACT.Exp, scale=FC_DESCALE).then_inc(s["b_ex"], 1)

            def b_g9(u):
                act.wait_ge(s["b_gT"], u + 1)
                copy(g9, bkX[0:EXP, :]).then_inc(s["b_g9"], 1)

            def b_bias(u, up):
                wait_past(act, "f_dd", Q * (u - 1))
                act.wait_ge(s["b_bias"], u + 1)
                copy(acc[up], bkZ[:, :]).then_inc(s["b_acc"], 1)

            def b_gelu(g, e, j):
                n = J * g + j
                act.wait_ge(s["b_fc"], n + 1)
                act.wait_ge(s["b_lo"], n + 1)
                act.activation(h32[j], bkF[j][:, :], ACT.Gelu_apprx_tanh, bias=pcol[:, e * J + j:e * J + j + 1],
                               scale=FC_DESCALE).then_inc(s["b_gelu"], 1)

            def b_tile(t, tp):
                for e in range(EXP):
                    if e == 0:
                        b_g9(t)
                    for j in range(J):
                        b_gelu(EXP * t + e, e, j)
                    if e == 0:
                        b_bias(t, tp)
                    if not is_int(t) or t + 1 < TILES:
                        b_piece(t + 1, e, 1 - tp)
                    if not is_int(t) or t + 2 < TILES:
                        g_piece(t + 2, e)

            for u in range(2):
                for e in range(EXP):
                    g_piece(u, e)
            for e in range(EXP):
                b_piece(0, e, 0)
            b_tile(0, 0)
            b_tile(1, 1)
            with act.Fori(1, PAIRS - 1) as i:
                b_tile(2 * i, 0)
                b_tile(2 * i + 1, 1)
            b_tile(TILES - 2, 0)
            b_tile(TILES - 1, 1)

        @block.vector
        def _(dve):
            def sub_scale(o, i, mean, rstd):
                return dve.tensor_scalar(o, i, mean, rstd, ALU.subtract, ALU.mult)

            dve.memset(xT[0][:, 0:1], 0.0).then_inc(s["xt0_zero"], 1)
            dve.memset(kv[0][:, 0:1], 0.0).then_inc(s["a_sel"], RS)
            dve.memset(kv[0][:, 1:2], 0.0).then_inc(s["b_lo"], J)
            dve.memset(kv[0][:, 2:3], 0.0).then_inc(s["b_proj"], 2)
            dve.memset(kv[0][:, 3:4], 0.0).then_inc(s["b_comb"], 2 * Q)

            def a_stats(t, par):
                wait_past(dve, "a_xn", Q * (t - 1))
                for q in range(Q):
                    dve.bn_stats(ast[:, 6 * q:6 * q + 6], chunk_of(xres, t, q)).then_inc(s["a_stats"], 1)
                wait_apart(dve, "a_stats", Q * t + Q)
                for q in range(Q):
                    dve.bn_aggr(amv[par][:, 2 * q:2 * q + 2], ast[:, 6 * q:6 * q + 6]).then_inc(s["a_mv"], 1)

            def a_xn(t, par):
                wait_past(dve, "a_xT_ps", t)
                dve.wait_ge(s["a_rstd"], t + 1)
                for q in range(Q):
                    sub_scale(xn[:, q * P:(q + 1) * P], chunk_of(xres, t, q), amv[par][:, 2 * q:2 * q + 1],
                              ars[par][:, q:q + 1]).then_inc(s["a_xn"], 1)

            def a_mix(t, par, n, col):
                if n == 0:
                    dve.wait_ge(s["a_xx"], t + 1)
                if n:
                    wait_past(dve, ("a_k_ps", "a_r_ps", "a_g_ps")[n - 1], t)
                dve.scalar_tensor_tensor(out=(xmix_v[par], xmix_k, xmix_r, xmix_g)[n], in0=xx, scalar=pcol[:, col:col + 1],
                                         in1=xT[par][:, 1:TOK + 1], op0=ALU.mult, op1=ALU.add).then_inc(s["a_mix"], 1)

            MIX = (MAA_V, MAA_K, MAA_R, MAA_G)

            def a_step(t, par, m):
                n = N * t + m
                if par:
                    dve.wait_ge(s["a_rs"], n - N + 1)
                    dve.tensor_copy(S[m][:, 0:1], S[m][:, TOK:TOK + 1]).then_inc(s["a_carry"], 1)
                else:
                    wait_past(dve, "a_rs", n - N + 1)
                    dve.memset(S[m][:, 0:1], 0.0).then_inc(s["a_carry"], 1)
                dve.wait_ge(s["a_vrep"], n + 1)
                if m == 0:
                    dve.wait_ge(s["a_k"], t + 1)
                dve.tensor_tensor(kv[m % 2], bkV[m % 2][:, :], kch[par], ALU.mult).then_inc(s["a_kv"], 1)
                dve.wait_ge(s["a_kv"], n + 1)
                dve.wait_ge(s["a_carry"], n + 1)
                dve.tensor_tensor_scan(S[m][:, 1:TOK + 1], wcol[:, 0:1].to_broadcast([P, TOK]), kv[m % 2],
                                       S[m][:, 0:1], ALU.mult, ALU.add).then_inc(s["a_scan"], 1)

            def a_yu(t):
                dve.wait_ge(s["a_vt"], t + 1)
                dve.wait_ge(s["a_rk"], t + 1)
                dve.tensor_tensor(tile_of(yres, t).rearrange("p (h m) -> p h m", m=N),
                                  bkA[:, :].rearrange("p (h m) -> p h m", m=N),
                                  rk.unsqueeze(2).to_broadcast([P, Q * H, N]), ALU.mult).then_inc(s["a_yu"], 1)

            def a_y(t):
                dve.wait_ge(s["a_yu"], t + 1)
                for b in range(2):
                    dve.wait_ge(s["a_yT"], 2 * t + b + 1)
                    y = tile_of(yres, t).rearrange("p (q h b g) -> p q h b g", h=H, b=2, g=4)[:, :, :, b, :]
                    ps = (bkC, bkD)[b][:, :].rearrange("p (q g h) -> p q h g", g=4, h=32)[:, :, 0:H, :]
                    dve.tensor_tensor(y, ps, y, ALU.add).then_inc(s["a_y"], 1)

            def a_tile(t, par):
                first, last, ending = (is_int(t) and v for v in (t == 0, t == TILES - 1, t >= TILES - 2))
                for m in range(N):
                    a_step(t, par, m)
                    if m == 0 and not last:
                        a_xn(t + 1, 1 - par)
                    if m == 1 and not first:
                        a_y(t - 1)
                    if m == 2:
                        a_yu(t)
                    if 3 <= m < 7 and not last:
                        a_mix(t + 1, 1 - par, m - 3, MIX[m - 3])
                    if m == 5 and not ending:
                        if is_int(t) and t == 0:
                            dve.wait_ge(s["x_second_in"], 16)
                        a_stats(t + 2, par)

            dve.wait_ge(s["x_first_in"], 16)
            a_stats(0, 0)
            a_xn(0, 0)
            a_stats(1, 1)
            dve.wait_ge(s["setup_ev"], 8)
            for m in range(N):
                src = wt[:, V_, :].rearrange("p (h m) -> p h m", m=N)[:, :, m:m + 1].to_broadcast([P, H, N])
                dve.tensor_copy(wvrep[:, m, :].rearrange("p (h n) -> p h n", n=N), src).then_inc(s["wvrep_done"], 1)
            dve.scalar_tensor_tensor(out=wrt_lo[:, :], in0=wrt[:, :], scalar=W_SCALE, in1=wrt_hi[:, :],
                                     op0=ALU.mult, op1=ALU.subtract).then_inc(s["wvrep_done"], 1)
            for n in range(4):
                a_mix(0, 0, n, MIX[n])
            dve.wait_ge(s["decay_r"], 2)
            a_tile(0, 0)
            a_tile(1, 1)
            dve.wait_ge(s["x_rest_in"], 16 * (B - 2))
            with dve.Fori(1, PAIRS - 1) as i:
                a_tile(2 * i, 0)
                a_tile(2 * i + 1, 1)
            a_tile(TILES - 2, 0)
            a_tile(TILES - 1, 1)
            a_y(TILES - 1)

            for i in range(2 * EXP):
                dve.wait_ge(s["split_hi"], i + 1)
                dve.scalar_tensor_tensor(out=w_lo(i), in0=w_stage(i), scalar=W_SCALE, in1=w_hi(i),
                                         op0=ALU.mult, op1=ALU.subtract).then_inc(s["split_lo"], 1)

            def stats(src, st, mv, s_st, s_mv, t):
                for q in range(Q):
                    dve.bn_stats(st[:, 6 * q:6 * q + 6], src(q)).then_inc(s[s_st], 1)
                wait_apart(dve, s_st, Q * t + Q)
                for q in range(Q):
                    dve.bn_aggr(mv[:, 2 * q:2 * q + 2], st[:, 6 * q:6 * q + 6]).then_inc(s[s_mv], 1)

            def normalise(dst, src, mv, rs, s_out):
                for q in range(Q):
                    sub_scale(dst[:, q * P:(q + 1) * P], src(q), mv[:, 2 * q:2 * q + 1],
                              rs[:, q:q + 1]).then_inc(s[s_out], 1)

            def per_expert(a):
                return a.rearrange("p (q e) -> p q e", e=E)

            def over_experts(a):
                return a.unsqueeze(2).to_broadcast([P, Q, E])

            def g_piece(u, e):
                y3 = tile_of(yres, u).rearrange("p (h m) -> p h m", m=N)
                if e == 0:
                    dve.tensor_reduce(s64, y3, AX.X, ALU.add).then_inc(s["g_s"], 1)
                    wait_past(dve, "g_yn", u)
                    dve.wait_ge(s["g_s"], u + 1)
                    dve.scalar_tensor_tensor(out=yc.rearrange("p (h m) -> p h m", m=N),
                                             in0=s64.unsqueeze(2).to_broadcast([P, Q * H, N]), scalar=-1.0 / N,
                                             in1=y3, op0=ALU.mult, op1=ALU.add).then_inc(s["g_yc"], 1)
                if e == 1:
                    dve.wait_ge(s["g_sq"], u + 1)
                    dve.tensor_reduce(v64, sq.rearrange("p (h m) -> p h m", m=N), AX.X, ALU.add).then_inc(s["g_v"], 1)
                if e == 2:
                    dve.wait_ge(s["g_ve"], u + 1)
                    dve.tensor_scalar(gshift, gve.bitcast(U32), 1, None, ALU.logical_shift_right)\
                       .then_inc(s["g_shift"], 1)
                    dve.wait_ge(s["g_shift"], u + 1)
                    dve.tensor_scalar(grs.bitcast(U32), gshift, -1.0, float(GUESS), ALU.mult, ALU.add)\
                       .then_inc(s["g_guess"], 1)

            def b_piece(u, e, up):
                if e == 2:
                    dve.wait_ge(s["b_o"], u + 1)
                    stats(lambda q: bkZ[:, q * P:(q + 1) * P], ost, omv, "b_ost", "b_omv", u)
                if e == 3:
                    dve.wait_ge(s["b_ors"], u + 1)
                    normalise(dd, lambda q: bkZ[:, q * P:(q + 1) * P], omv, ors, "b_dd")
                if e == 4:
                    dve.wait_ge(s["b_x1"], u + 1)
                    stats(lambda q: chunk_of(xres, u, q), xst, xmv, "b_xst", "b_xmv", u)
                if e == 5:
                    dve.wait_ge(s["b_xrs"], u + 1)
                    normalise(xn2, lambda q: chunk_of(xres, u, q), xmv, xrs, "b_xn2")
                if e == 6:
                    dve.wait_ge(s["b_xh"], u + 1)
                    dve.scalar_tensor_tensor(out=xl[up], in0=bkX[:, :], scalar=X_SCALE, in1=xh[up],
                                             op0=ALU.mult, op1=ALU.subtract).then_inc(s["b_xl"], 1)
                if e == 7:
                    dve.wait_ge(s["b_lg"], u + 1)
                    z3 = bkZ[:, 0:Q * E].rearrange("p (q e) -> p q e", e=E)
                    dve.tensor_reduce(mx, z3, AX.X, ALU.max).then_inc(s["b_mx"], 1)
                    dve.wait_ge(s["b_mx"], u + 1)
                    dve.tensor_tensor(per_expert(lg), z3, over_experts(mx), ALU.subtract).then_inc(s["b_lgd"], 1)
                if e == 8:
                    dve.wait_ge(s["b_ex"], u + 1)
                    dve.tensor_reduce(se, per_expert(ex), AX.X, ALU.add).then_inc(s["b_se"], 1)
                    dve.wait_ge(s["b_se"], u + 1)
                    dve.reciprocal(rse, se).then_inc(s["b_rse"], 1)
                    dve.wait_ge(s["b_rse"], u + 1)
                    dve.tensor_tensor(per_expert(pr), per_expert(ex), over_experts(rse), ALU.mult)\
                       .then_inc(s["b_pr"], 1)
                    wait_apart(dve, "b_pr", u + 1)
                    for q in range(Q):
                        dve.max(top[:, 8 * q:8 * q + 8], pr[:, E * q:E * q + E]).then_inc(s["b_top"], 1)
                    wait_apart(dve, "b_top", Q * u + Q)
                    for q in range(Q):
                        dve.max_index(tix[:, 8 * q:8 * q + 8], top[:, 8 * q:8 * q + 8], pr[:, E * q:E * q + E])\
                           .then_inc(s["b_tix"], 1)
                    top3 = top.rearrange("p (q k) -> p q k", k=8)
                    dve.tensor_tensor(s2.unsqueeze(2), top3[:, :, 0:1], top3[:, :, 1:2], ALU.add)\
                       .then_inc(s["b_s2"], 1)
                    dve.wait_ge(s["b_s2"], u + 1)
                    dve.reciprocal(r2, s2).then_inc(s["b_r2"], 1)
                    dve.wait_ge(s["b_tix"], Q * u + Q)
                    dve.tensor_copy(tif, tix).then_inc(s["b_eq"], 1)
                    dve.wait_ge(s["b_r2"], u + 1)
                    g23 = g2.rearrange("p (q k) -> p q k", k=2)
                    dve.scalar_tensor_tensor(out=g23, in0=top3[:, :, 0:2], scalar=PROJ_DESCALE,
                                             in1=r2.unsqueeze(2).to_broadcast([P, Q, 2]), op0=ALU.mult,
                                             op1=ALU.mult).then_inc(s["b_g2"], 1)
                    dve.wait_ge(s["b_eq"], 5 * u + 1)
                    tif3 = tif.rearrange("p (q k) -> p q k", k=8)
                    io = iota8[:, :].unsqueeze(1).to_broadcast([P, Q, E])
                    for k in range(2):
                        dve.tensor_tensor(per_expert(eq[k]), io, tif3[:, :, k:k + 1].to_broadcast([P, Q, E]),
                                          ALU.is_equal).then_inc(s["b_eq"], 1)
                    dve.wait_ge(s["b_g2"], u + 1)
                    for k in range(2):
                        dve.wait_ge(s["b_eq"], 5 * u + 2 + k)
                        dve.tensor_tensor(per_expert(eq[k]), per_expert(eq[k]),
                                          g23[:, :, k:k + 1].to_broadcast([P, Q, E]), ALU.mult)\
                           .then_inc(s["b_eq"], 1)
                    dve.wait_ge(s["b_eq"], 5 * u + 5)
                    dve.tensor_tensor(gates[up][:, :, 0:E], per_expert(eq[0]), per_expert(eq[1]), ALU.add)\
                       .then_inc(s["b_gate"], 1)

            def b_lo(g, j, par):
                n = J * g + j
                dve.wait_ge(s["b_hi"], n + 1)
                dve.scalar_tensor_tensor(out=hl[par][j], in0=h32[j], scalar=H_SCALE, in1=hh[par][j],
                                         op0=ALU.mult, op1=ALU.subtract).then_inc(s["b_lo"], 1)

            def b_comb(t, g, e, tp, par):
                dve.wait_ge(s["b_proj"], g + 1 + 2)
                if e == 0:
                    dve.wait_ge(s["b_acc"], t + 1)
                for q in range(Q):
                    a = acc[tp][:, q * P:(q + 1) * P]
                    dve.wait_ge(s["b_comb"], Q * g + q + 1 - Q + 2 * Q)
                    dve.scalar_tensor_tensor(out=a, in0=bkP[par][:, q * P:(q + 1) * P],
                                             scalar=gates[tp][:, q, e:e + 1], in1=a,
                                             op0=ALU.mult, op1=ALU.add).then_inc(s["b_comb"], 1)

            def f_stats(t, tp):
                dve.wait_ge(s["b_comb"], Q * EXP * (t + 1) + 2 * Q)
                stats(lambda q: acc[tp][:, q * P:(q + 1) * P], fst, fmv, "f_st", "f_mv", t)

            def f_norm(t, tp):
                dve.wait_ge(s["f_rs"], t + 1)
                wait_past(dve, "f_ob", t)
                normalise(dd2, lambda q: acc[tp][:, q * P:(q + 1) * P], fmv, frs, "f_dd")

            def b_tile(t, tp):
                for e in range(EXP):
                    g = EXP * t + e
                    par = (EXP * tp + e) % 2
                    for j in range(J):
                        b_lo(g, j, par)
                    if e:
                        b_comb(t, g - 1, e - 1, tp, 1 - par)
                    if not is_int(t) or t > 0:
                        if e == 0:
                            b_comb(t - 1, g - 1, EXP - 1, 1 - tp, 1 - par)
                            f_stats(t - 1, 1 - tp)
                        if e == 1:
                            f_norm(t - 1, 1 - tp)
                    if not is_int(t) or t + 1 < TILES:
                        b_piece(t + 1, e, 1 - tp)
                    if not is_int(t) or t + 2 < TILES:
                        g_piece(t + 2, e)

            for u in range(2):
                for e in range(EXP):
                    g_piece(u, e)
            for e in range(EXP):
                b_piece(0, e, 0)
            b_tile(0, 0)
            b_tile(1, 1)
            with dve.Fori(1, PAIRS - 1) as i:
                b_tile(2 * i, 0)
                b_tile(2 * i + 1, 1)
            b_tile(TILES - 2, 0)
            b_tile(TILES - 1, 1)
            b_comb(TILES - 1, EXP * TILES - 1, EXP - 1, 1, (EXP * TILES - 1) % 2)
            f_stats(TILES - 1, 1)
            f_norm(TILES - 1, 1)

        @block.tensor
        def _(pe):
            def mm(o, lhsT, rhs, start=True, stop=True, **k):
                return pe.matmul(o, lhsT, rhs, start=start, stop=stop, **k)

            pe.wait_ge(s["const"], 7)
            pe.wait_ge(s["params_in"], N_PARAMS)
            mm(bkV[0][:, 0:2], selT[:, :], dcol[:, :]).then_inc(s["decay_ps"], 1)
            for n in range(5):
                if n >= 4:
                    pe.wait_ge(s["setup_ev"], n - 3)
                pe.transpose(bank[n % 4][:, 0:C], wraw[n], ident[:, :]).then_inc(s["setup_t"], 1)
            pe.transpose(bkV[1][:, 0:NB], prow, ident[0:NB, 0:NB]).then_inc(s["setup_t"], 1)

            def a_T(t):
                pe.wait_ge(s["a_xn"], Q * t + Q)
                wait_past(pe, "a_yu", t - 1)
                for q in range(Q):
                    i = pe.transpose(bkA[:, q * P:(q + 1) * P], xn[:, q * P:(q + 1) * P], ident[:, :])
                i.then_inc(s["a_xT_ps"], 1)

            def a_kr(t, par):
                pe.wait_ge(s["a_mix"], 4 * t + 2)
                wait_past(pe, "a_y", 2 * t - 2)
                mm(bkC[:, :], wt[:, K_, :], xmix_k).then_inc(s["a_k_ps"], 1)
                pe.wait_ge(s["a_mix"], 4 * t + 3)
                wait_past(pe, "a_rk", t)
                mm(bkB[:, :], wt[:, R_, :], xmix_r).then_inc(s["a_r_ps"], 1)

            def a_g(t, par):
                pe.wait_ge(s["a_mix"], 4 * t + 4)
                mm(bkD[:, :], wt[:, G_, :], xmix_g).then_inc(s["a_g_ps"], 1)

            def a_vrep(t, par, m, lead):
                if not lead:
                    pe.wait_ge(s["a_kv"], N * t + m - 1)
                mm(bkV[m % 2][:, :], wvrep[:, m, :], xmix_v[par]).then_inc(s["a_vrep"], 1)

            def a_sel(t, m):
                if m == 0:
                    wait_past(pe, "a_yev", 2 * t)
                pe.wait_ge(s["a_rs"], N * t + m + 1)
                g = 32 * (m % 4)
                mm(bkY[m // 4][g:g + 32, :], sel[:, :], rS[m % RS]).then_inc(s["a_sel"], 1)

            def a_vtok(t, par, last):
                pe.wait_ge(s["a_xT"], t + 1 if last else t + 2)
                for q in range(Q):
                    i = mm(bkA[:, q * P:(q + 1) * P], xmix_v[par][:, q * P:(q + 1) * P], wt[:, V_, :])
                i.then_inc(s["a_vt"], 1)

            def a_rk(t):
                pe.wait_ge(s["a_ruk"], t + 1)
                for q in range(Q):
                    i = mm(bkB[:, q * H:(q + 1) * H], ruk[:, q * P:(q + 1) * P], sel[:, 0:H])
                i.then_inc(s["a_rk_ps"], 1)

            def a_yT(t, last):
                for b in range(2):
                    pe.wait_ge(s["a_yev"], 2 * t + b + 1)
                    pe.wait_ge(s["a_g" if b else "a_uk"], t + 1 if last else t + 2)
                    for q in range(Q):
                        i = pe.transpose((bkC, bkD)[b][:, q * P:(q + 1) * P], ych[b][:, q * P:(q + 1) * P],
                                         ident[:, :])
                    i.then_inc(s["a_yT"], 1)

            def a_tile(t, par, last):
                for m in range(N):
                    if m + 2 < N:
                        a_vrep(t, par, m + 2, False)
                    elif not last:
                        a_vrep(t + 1, 1 - par, m + 2 - N, False)
                    if m > 0:
                        a_sel(t, m - 1)
                    if m == 0 and not last:
                        a_T(t + 1)
                    if m == 1:
                        a_vtok(t, par, last)
                    if m == 2:
                        a_rk(t)
                    if m == 5 and not last:
                        a_kr(t + 1, 1 - par)
                if not last:
                    a_g(t + 1, 1 - par)
                a_sel(t, N - 1)
                a_yT(t, last)

            pe.wait_ge(s["setup_ev"], 8)
            pe.wait_ge(s["decay_r"], 2)
            a_T(0)
            a_kr(0, 0)
            a_g(0, 0)
            pe.wait_ge(s["wvrep_done"], N + 1)
            a_vrep(0, 0, 0, True)
            a_vrep(0, 0, 1, True)
            a_tile(0, 0, False)
            a_tile(1, 1, False)
            with pe.Fori(1, PAIRS - 1) as i:
                a_tile(2 * i, 0, False)
                a_tile(2 * i + 1, 1, False)
            a_tile(TILES - 2, 0, False)
            a_tile(TILES - 1, 1, True)

            def b_piece(u, e, up):
                if e == 1:
                    wait_past(pe, "b_g9", u)
                    pe.wait_ge(s["g_yn"], u + 1)
                    for q in range(Q):
                        i = pe.transpose(bkX[:, q * P:(q + 1) * P], yn[up][:, q * P:(q + 1) * P], ident[:, :])
                    i.then_inc(s["b_ynT"], 1)
                if e == 2:
                    wait_past(pe, "b_acc", u)
                    pe.wait_ge(s["b_zz"], u + 1)
                    for q in range(Q):
                        i = mm(bkZ[:, q * P:(q + 1) * P], zz[:, q * P:(q + 1) * P], wt[:, O_, :])
                    i.then_inc(s["b_o"], 1)
                if e == 6:
                    pe.wait_ge(s["b_xn2"], Q * u + Q)
                    for q in range(Q):
                        i = pe.transpose(bkX[:, q * P:(q + 1) * P], xn2[:, q * P:(q + 1) * P], ident[:, :])
                    i.then_inc(s["b_xn2T"], 1)
                if e == 7:
                    pe.wait_ge(s["b_xl"], u + 1)
                    for q in range(Q):
                        xs = slice(q * P, (q + 1) * P)
                        o = bkZ[:, q * E:(q + 1) * E]
                        mm(o, xh[up][:, xs], wrt_lo[:, :], True, False)
                        mm(o, xl[up][:, xs], wrt_hi[:, :], False, False)
                        i = mm(o, xh[up][:, xs], wrt_hi[:, :], False, True)
                    i.then_inc(s["b_lg"], 1)

            def b_gT(u, up):
                pe.wait_ge(s["b_gate"], u + 1)
                for q in range(Q):
                    i = pe.transpose(bkX[0:EXP, q * P:(q + 1) * P], gates[up][:, q, :], ident[:, :])
                i.then_inc(s["b_gT"], 1)

            def b_bias(u):
                pe.wait_ge(s["b_g9"], u + 1)
                for q in range(Q):
                    i = mm(bkZ[:, q * P:(q + 1) * P], g9[:, q * P:(q + 1) * P], bps[:, :])
                i.then_inc(s["b_bias"], 1)

            def b_fc(g, e, up, lead):
                for j in range(J):
                    if not lead:
                        pe.wait_ge(s["b_gelu"], J * (g - 1) + j + 1)
                    js = slice(j * P, (j + 1) * P)
                    mm(bkF[j][:, :], w_lo(e)[:, js], xh[up], True, False)
                    mm(bkF[j][:, :], w_hi(e)[:, js], xl[up], False, False)
                    mm(bkF[j][:, :], w_hi(e)[:, js], xh[up], False, True).then_inc(s["b_fc"], 1)

            def b_proj(g, e, par):
                pe.wait_ge(s["b_lo"], J * (g + 1) + J)
                pe.wait_ge(s["b_comb"], Q * (g + 1))
                for q in range(Q):
                    o = bkP[par][:, q * P:(q + 1) * P]
                    qs = slice(q * P, (q + 1) * P)
                    for j in range(J):
                        js = slice(j * P, (j + 1) * P)
                        mm(o, hl[par][j][:, qs], w_hi(EXP + e)[:, js], j == 0, False)
                        mm(o, hh[par][j][:, qs], w_lo(EXP + e)[:, js], False, False)
                        i = mm(o, hh[par][j][:, qs], w_hi(EXP + e)[:, js], False, j == J - 1)
                i.then_inc(s["b_proj"], 1)

            def b_tile(t, tp):
                last = is_int(t) and t + 1 == TILES
                for e in range(EXP):
                    g = EXP * t + e
                    if not last:
                        b_piece(t + 1, e, 1 - tp)
                    if e == 0:
                        b_gT(t, tp)
                    if e + 1 < EXP:
                        b_fc(g + 1, e + 1, tp, False)
                    elif not last:
                        b_fc(g + 1, 0, 1 - tp, False)
                    if e == 0:
                        b_bias(t)
                    b_proj(g, e, (EXP * tp + e) % 2)

            pe.wait_ge(s["a_y"], 2 * TILES)
            for e in range(EXP):
                b_piece(0, e, 0)
            pe.wait_ge(s["split_lo"], 2 * EXP)
            b_fc(0, 0, 0, True)
            b_tile(0, 0)
            b_tile(1, 1)
            with pe.Fori(1, PAIRS - 1) as i:
                b_tile(2 * i, 0)
                b_tile(2 * i + 1, 1)
            b_tile(TILES - 2, 0)
            b_tile(TILES - 1, 1)


_INS = ['L0_attn_x', 'L0_attn_time_maa_k', 'L0_attn_time_maa_v', 'L0_attn_time_maa_r', 'L0_attn_time_maa_g',
        'L0_attn_time_decay', 'L0_attn_time_faaaa', 'L0_attn_Wr', 'L0_attn_Wk', 'L0_attn_Wv', 'L0_attn_Wg',
        'L0_attn_Wo', 'L0_attn_ln_w', 'L0_attn_ln_b', 'L0_ffn_Wfc_s', 'L0_ffn_bfc_s', 'L0_ffn_Wproj_s',
        'L0_ffn_bproj_s', 'L0_ffn_Wr', 'L0_ffn_Wfc', 'L0_ffn_bfc', 'L0_ffn_Wproj', 'L0_ffn_bproj']
_OUT = (8, 1024, 128)


def kernel(**inputs):
    import numpy as _np
    import concourse.bacc as _bacc
    from concourse.bass_utils import run_bass_kernel_spmd as _run

    nc = _bacc.Bacc("TRN2", target_bir_lowering=False, num_devices=1)
    arrays, args = {}, []
    for name in _INS:
        a = _np.ascontiguousarray(inputs[name])
        arrays[f"in_{name}"] = a
        args.append(nc.dram_tensor(f"in_{name}", a.shape, mybir.dt.from_np(a.dtype), kind="ExternalInput").ap())
    args.append(nc.dram_tensor("out_0", _OUT, F32, kind="ExternalOutput").ap())
    build(nc, *args)
    r = _run(nc, [arrays], core_ids=[0])
    return r.results[0]["out_0"]
```

```python
import concourse.bass as bass
from concourse import mybir
from contextlib import ExitStack

F32 = mybir.dt.float32
F16 = mybir.dt.float16
U32 = mybir.dt.uint32
ALU = mybir.AluOpType
ACT = mybir.ActivationFunctionType
AX = mybir.AxisListType

B, T, C = 8, 1024, 128
H, N = 16, 8
P = 128
TOK = 512
Q = TOK // P
TILES = B * T // TOK
PAIRS = TILES // 2
E = 8
EXP = E + 1
HID = 512
J = HID // P
EPS_LN = 1e-5
EPS_GN = 1e-5 * 64
W_SCALE = 2.0 ** 8
X_SCALE = 2.0 ** 8
H_SCALE = 2.0 ** 6
FC_DESCALE = 1.0 / (W_SCALE * X_SCALE)
PROJ_DESCALE = 1.0 / (H_SCALE * W_SCALE)
NEWTON = 3
GUESS = 0x5F3759DF
R_, K_, V_, G_, O_ = range(5)
NB_BFC = EXP * J
NB = NB_BFC + 6
MAA_K, MAA_V, MAA_R, MAA_G, LN_W, LN_B = range(NB_BFC, NB)
RS = 4
SPLIT_AHEAD = 12
CH = 512


def is_int(t):
    return isinstance(t, int)


def build(nc, x, maa_k, maa_v, maa_r, maa_g, decay, faaaa, wr, wk, wv, wg, wo, ln_w, ln_b,
          wfc_s, bfc_s, wproj_s, bproj_s, w_router, wfc, bfc, wproj, bproj, out):
    ctx = ExitStack()
    with ctx:
        def sb(name, shape, dt=F32):
            return ctx.enter_context(nc.sbuf_tensor(name, shape, dt))

        def sem(name):
            return ctx.enter_context(nc.semaphore(name))

        xres = sb("xres", [P, TILES * TOK])
        yres = sb("yres", [P, TILES * TOK])
        gres = sb("gres", [P, TILES * TOK])
        wexp = sb("wexp", [P, (2 * EXP + 1) * CH])
        wt = sb("wt", [P, 5, C])
        wvrep = sb("wvrep", [P, N, P])
        ident = sb("ident", [P, P])
        sel = sb("sel", [P, 32])
        selT = sb("selT", [H, P])
        pcol = sb("pcol", [P, NB])
        wcol = sb("wcol", [P, 1])
        ucol = sb("ucol", [P, 1])
        neghalf = sb("neghalf", [P, Q])
        iota8 = sb("iota8", [P, E])
        wrt = sb("wrt", [P, E])
        wrt_hi = sb("wrt_hi", [P, E], F16)
        wrt_lo = sb("wrt_lo", [P, E], F16)
        bprow = sb("bprow", [EXP, C])
        bps = sb("bps", [EXP, C])
        dcol = sb("dcol", [H, 2])
        gates = [sb(f"gates{i}", [P, Q, EXP]) for i in range(2)]

        WORK = 16400
        work = sb("work", [P, WORK])
        cut_at = [0]

        def cut(n, dt=F32):
            words = n if dt == F32 else n // 2
            a = cut_at[0]
            cut_at[0] += words
            assert cut_at[0] <= WORK, cut_at
            v = work[:, a:a + words]
            return v if dt == F32 else v.bitcast(dt)

        xn = cut(TOK)
        xT = [cut(TOK + 1) for _ in range(2)]
        cut_at[0] += cut_at[0] % 2
        xx = cut(TOK)
        xmix_k, xmix_r, xmix_g = (cut(TOK) for _ in range(3))
        xmix_v = [cut(TOK) for _ in range(2)]
        kch = [cut(TOK) for _ in range(2)]
        rch = [cut(TOK) for _ in range(2)]
        kv = [cut(TOK) for _ in range(2)]
        S_AT = cut_at[0]
        wraw = [cut(C) for _ in range(5)]
        prow = cut(C)[0:NB, :]
        dexp = cut(2)
        cut_at[0] = S_AT
        S = [cut(TOK + 2) for _ in range(N)]
        rS = [cut(TOK) for _ in range(RS)]
        uk = cut(TOK)
        ruk = cut(TOK)
        ych = [cut(TOK) for _ in range(2)]
        rk = cut(Q * H)
        ast = cut(Q * 6)
        amv = [cut(Q * 2) for _ in range(2)]
        ave = cut(Q)
        ars = cut(Q)
        anm = cut(Q)
        anmr = cut(Q)
        A_END = cut_at[0]
        cut_at[0] = 0
        s64 = cut(Q * H)
        v64 = cut(Q * H)
        gve = cut(Q * H)
        ghv = cut(Q * H)
        gshift = cut(Q * H).bitcast(U32)
        grs = cut(Q * H)
        gsq = cut(Q * H)
        gtm = cut(Q * H)
        gtf = cut(Q * H)
        yc = cut(TOK)
        sq = cut(TOK)
        yn = [cut(TOK) for _ in range(2)]
        zT = cut(TOK)
        zz = cut(TOK)
        dd = cut(TOK)
        xn2 = cut(TOK)
        xh = [cut(TOK, F16) for _ in range(2)]
        xl = [cut(TOK, F16) for _ in range(2)]
        h32 = [cut(TOK) for _ in range(J)]
        hh = [[cut(TOK, F16) for _ in range(J)] for _ in range(2)]
        hl = [[cut(TOK, F16) for _ in range(J)] for _ in range(2)]
        acc = [cut(TOK) for _ in range(2)]
        dd2 = cut(TOK)
        ob = cut(TOK)
        g9 = cut(TOK)[0:EXP, :]
        ost = cut(Q * 6)
        omv = cut(Q * 2)
        ove = cut(Q)
        ors = cut(Q)
        xst = cut(Q * 6)
        xmv = cut(Q * 2)
        xve = cut(Q)
        xrs = cut(Q)
        fst = cut(Q * 6)
        fmv = cut(Q * 2)
        fve = cut(Q)
        frs = cut(Q)
        mx = cut(Q)
        lg = cut(Q * E)
        ex = cut(Q * E)
        se = cut(Q)
        rse = cut(Q)
        pr = cut(Q * E)
        top = cut(Q * 8)
        tix = cut(Q * 8).bitcast(U32)
        tif = cut(Q * 8)
        s2 = cut(Q)
        r2 = cut(Q)
        g2 = cut(Q * 2)
        eq = [cut(Q * E) for _ in range(2)]

        bank = [ctx.enter_context(nc.psum_tensor(f"bank{i}", [P, 512], F32)) for i in range(8)]

        s = {n: sem(n) for n in (
            "params_in wexp_in x_first_in x_second_in x_rest_in out_done "
            "const pool_set setup_t setup_ev decay_ps decay_e decay_r wvrep_done xt0_zero split_s split_hi split_lo "
            "a_stats a_mv a_ve a_rstd a_nm a_nmr a_xn a_xT_ps a_xT a_edge a_xx a_mix a_k_ps a_r_ps a_g_ps a_k a_uk a_r a_g "
            "a_vrep a_kv a_carry a_scan a_rs a_sel a_yev a_vt a_ruk a_rk_ps a_rk a_yu a_yT a_y "
            "g_s g_yc g_sq g_v g_ve g_hv g_shift g_guess g_newton g_yn b_ynT b_zT b_zz b_o b_ost b_omv b_ove b_ors b_dd b_x1 "
            "b_xst b_xmv b_xve b_xrs b_xn2 b_xn2T b_xh b_xl b_lg b_mx b_lgd b_ex b_se b_rse b_pr b_top b_tix "
            "b_s2 b_r2 b_g2 b_eq b_gate b_gT b_g9 b_bias b_acc "
            "b_fc b_gelu b_hi b_lo b_proj b_comb f_st f_mv f_ve f_rs f_dd f_ob").split()}

        bkA, bkB, bkC, bkD = bank[7], bank[6], bank[2], bank[3]
        bkV, bkY = bank[4:6], bank[0:2]
        bkF, bkP, bkX, bkZ = bank[0:4], bank[4:6], bank[6], bank[7]

        def tile_of(res, t):
            return res[:, bass.ts(t, TOK)]

        def chunk_of(res, t, q):
            return res[:, bass.ds(t * TOK + q * P, P)]

        def fc(e):
            return 2 * e

        def proj(e):
            return 2 * e + 1

        def w_hi(i):
            return wexp[:, i * CH:i * CH + CH // 2].bitcast(F16)

        def w_lo(i):
            return wexp[:, i * CH + CH // 2:(i + 1) * CH].bitcast(F16)

        def w_stage(i):
            return wexp[:, (i + 1) * CH:(i + 2) * CH]

        def chunks_at(e):
            return range(SPLIT_AHEAD + e, min(SPLIT_AHEAD + e + 1, 2 * EXP))

        def wait_past(eng, name, value):
            if not isinstance(value, int) or value > 0:
                eng.wait_ge(s[name], value)

        def wait_apart(eng, name, value):
            if not isinstance(value, int):
                eng.to_reg(value)
            eng.wait_ge(s["const"], 1)
            eng.wait_ge(s[name], value)

        block = ctx.enter_context(nc.Block())

        @block.sync
        def _(sp):
            for i, w in enumerate((wr, wk, wv, wg, wo)):
                sp.dma_start(wraw[i], w).then_inc(s["params_in"], 16)
            sp.dma_start(prow[0:E * J, :], bfc.rearrange("e (j p) -> (e j) p", p=P)).then_inc(s["params_in"], 16)
            sp.dma_start(prow[E * J:NB_BFC, :], bfc_s.rearrange("(j p) -> j p", p=P)).then_inc(s["params_in"], 16)
            for r, m in ((MAA_K, maa_k), (MAA_V, maa_v), (MAA_R, maa_r), (MAA_G, maa_g)):
                sp.dma_start(prow[r:r + 1, :], m.rearrange("a b c -> (a b) c")).then_inc(s["params_in"], 16)
            for r, m in ((LN_W, ln_w), (LN_B, ln_b)):
                sp.dma_start(prow[r:r + 1, :], m.rearrange("(a c) -> a c", a=1)).then_inc(s["params_in"], 16)
            sp.dma_start(dcol[:, 0:1], decay).then_inc(s["params_in"], 16)
            sp.dma_start(dcol[:, 1:2], faaaa).then_inc(s["params_in"], 16)
            sp.dma_start(wrt[:, :], w_router).then_inc(s["params_in"], 16)
            sp.dma_start(bprow[0:E, :], bproj).then_inc(s["params_in"], 16)
            sp.dma_start(bprow[E:EXP, :], bproj_s.rearrange("(a c) -> a c", a=1)).then_inc(s["params_in"], 16)
            xv = x.rearrange("b (k p) c -> p b k c", p=P)
            xd = xres[:, :].rearrange("p (b k c) -> p b k c", b=B, c=C)
            sp.dma_start(xd[:, 0, :, :], xv[:, 0, :, :]).then_inc(s["x_first_in"], 16)
            for b in range(1, B):
                sp.dma_start(xd[:, b, :, :], xv[:, b, :, :]).then_inc(s["x_second_in" if b == 1 else "x_rest_in"], 16)
            for e in range(EXP):
                sp.dma_start(w_stage(fc(e)), wfc[e] if e < E else wfc_s).then_inc(s["wexp_in"], 16)
                src = wproj[e] if e < E else wproj_s
                sp.dma_start(w_stage(proj(e)).rearrange("p (j c) -> p j c", c=C),
                             src.rearrange("(j p) c -> p j c", p=P)).then_inc(s["wexp_in"], 16)

            with sp.Fori(0, PAIRS) as i:
                for half in range(2):
                    sp.wait_ge(s["f_ob"], 2 * i + half + 1)
                    sp.dma_start(out[bass.ds(i, 1), half * TOK:(half + 1) * TOK, :]
                                 .rearrange("b (k p) c -> p (b k) c", p=P),
                                 ob.rearrange("p (k c) -> p k c", c=C)).then_inc(s["out_done"], 16)
            sp.wait_ge(s["out_done"], 16 * TILES)

        N_PARAMS = 16 * (5 + 2 + 4 + 2 + 3 + 2)

        @block.gpsimd
        def _(pool):
            pool.memset(ident[:, :], 0.0).then_inc(s["pool_set"], 1)
            pool.memset(sel[:, :], 1.0).then_inc(s["pool_set"], 1)
            pool.memset(selT[:, :], 1.0).then_inc(s["pool_set"], 1)
            pool.memset(neghalf[:, :], -0.5).then_inc(s["const"], 1)
            pool.iota(iota8[:, :], pattern=[[1, E]], base=0, channel_multiplier=0,
                      allow_small_or_imprecise_dtypes=True).then_inc(s["const"], 1)
            for i in range(2):
                pool.memset(gates[i][:, :, E:EXP], PROJ_DESCALE).then_inc(s["const"], 1)
            pool.wait_ge(s["pool_set"], 3)
            pool.affine_select(out=ident[:, :], in_=ident[:, :], compare_op=ALU.not_equal, fill=1.0,
                               base=0, pattern=[[-1, P]], channel_multiplier=1).then_inc(s["const"], 1)
            pool.affine_select(out=sel[:, :], in_=sel[:, :], compare_op=ALU.is_ge, fill=0.0,
                               base=0, pattern=[[-N, 32]], channel_multiplier=1).then_inc(s["pool_set"], 1)
            pool.affine_select(out=selT[:, :], in_=selT[:, :], compare_op=ALU.is_ge, fill=0.0,
                               base=0, pattern=[[1, P]], channel_multiplier=-N).then_inc(s["pool_set"], 1)
            pool.wait_ge(s["pool_set"], 5)
            pool.affine_select(out=sel[:, :], in_=sel[:, :], compare_op=ALU.is_ge, fill=0.0,
                               base=N - 1, pattern=[[N, 32]], channel_multiplier=-1).then_inc(s["const"], 1)
            pool.affine_select(out=selT[:, :], in_=selT[:, :], compare_op=ALU.is_ge, fill=0.0,
                               base=N - 1, pattern=[[-1, P]], channel_multiplier=N).then_inc(s["const"], 1)

            def rsqrt(var, ve, rs, eps, s_in, n_in, s_ve, s_rs, t):
                wait_apart(pool, s_in, n_in)
                pool.tensor_scalar(ve, var, 1.0, eps, ALU.mult, ALU.add).then_inc(s[s_ve], 1)
                pool.wait_ge(s[s_ve], t + 1)
                pool.tensor_tensor(rs, ve, neghalf[:, :], ALU.pow).then_inc(s[s_rs], 1)

            def variance(mv):
                return mv.rearrange("p (q two) -> p q two", two=2)[:, :, 1]

            def a_rstd(t, par):
                wait_past(pool, "a_xn", Q * t)
                rsqrt(variance(amv[par]), ave, ars, EPS_LN, "a_mv", Q * t + Q, "a_ve", "a_rstd", t)
                pool.tensor_scalar(anm, amv[par].rearrange("p (q two) -> p q two", two=2)[:, :, 0], -1.0, 0.0,
                                   ALU.mult, ALU.add).then_inc(s["a_nm"], 1)
                pool.wait_ge(s["a_rstd"], t + 1)
                pool.wait_ge(s["a_nm"], t + 1)
                pool.tensor_tensor(anmr, anm, ars, ALU.mult).then_inc(s["a_nmr"], 1)

            def a_shift(t, par, pair):
                pool.wait_ge(s["a_xT"], t + 1)
                if par:
                    pool.wait_ge(s["a_edge"], pair + 1)
                pool.tensor_tensor(xx, xT[par][:, 0:TOK], xT[par][:, 1:TOK + 1], ALU.subtract).then_inc(s["a_xx"], 1)

            def a_rs(t, par, m):
                n = N * t + m
                pool.wait_ge(s["a_sel"], n + 1)
                if m == 0:
                    pool.wait_ge(s["a_r"], t + 1)
                pool.wait_ge(s["a_scan"], n + 1)
                pool.tensor_tensor(rS[m % RS], S[m][:, 0:TOK], rch[par], ALU.mult).then_inc(s["a_rs"], 1)

            def a_ruk(t, par):
                wait_past(pool, "a_rk_ps", t)
                pool.wait_ge(s["a_r"], t + 1)
                pool.wait_ge(s["a_uk"], t + 1)
                pool.tensor_tensor(ruk, uk, rch[par], ALU.mult).then_inc(s["a_ruk"], 1)

            def a_tile(pair, par):
                t = 2 * pair + par
                last, ending = (is_int(t) and v for v in (t == TILES - 1, t >= TILES - 2))
                for m in range(N):
                    if m == 7 and not last:
                        a_ruk(t + 1, 1 - par)
                    if m == 0 and not last:
                        a_shift(t + 1, 1 - par, pair)
                    a_rs(t, par, m)
                    if last and m >= 2:
                        g_piece(0, m, 0)
                    if m == 3 and not ending:
                        a_rstd(t + 2, par)

            def g_piece(u, e, up):
                if e == 2:
                    wait_apart(pool, "g_v", u + 1)
                    pool.tensor_scalar(gve, v64, 1.0 / N, EPS_GN, ALU.mult, ALU.add).then_inc(s["g_ve"], 1)
                    wait_apart(pool, "g_ve", u + 1)
                    pool.tensor_scalar(ghv, gve, -0.5, 0.0, ALU.mult, ALU.add).then_inc(s["g_hv"], 1)
                if 3 <= e < 3 + NEWTON:
                    n = 4 * NEWTON * u + 4 * (e - 3)
                    if e == 3:
                        pool.wait_ge(s["g_guess"], u + 1)
                        pool.wait_ge(s["g_hv"], u + 1)
                    else:
                        pool.wait_ge(s["g_newton"], n)
                    pool.tensor_tensor(gsq, grs, grs, ALU.mult).then_inc(s["g_newton"], 1)
                    pool.wait_ge(s["g_newton"], n + 1)
                    pool.tensor_tensor(gtm, gsq, ghv, ALU.mult).then_inc(s["g_newton"], 1)
                    wait_apart(pool, "g_newton", n + 2)
                    pool.tensor_scalar(gtf, gtm, 1.0, 1.5, ALU.mult, ALU.add).then_inc(s["g_newton"], 1)
                    pool.wait_ge(s["g_newton"], n + 3)
                    pool.tensor_tensor(grs, grs, gtf, ALU.mult).then_inc(s["g_newton"], 1)
                if e == 3 + NEWTON:
                    wait_past(pool, "b_ynT", u - 1)
                    pool.wait_ge(s["g_newton"], 4 * NEWTON * (u + 1))
                    pool.tensor_tensor(yn[up].rearrange("p (h m) -> p h m", m=N),
                                       yc.rearrange("p (h m) -> p h m", m=N),
                                       grs.unsqueeze(2).to_broadcast([P, Q * H, N]), ALU.mult).then_inc(s["g_yn"], 1)

            def b_gate(u):
                pool.wait_ge(s["b_zT"], u + 1)
                pool.tensor_tensor(zz, zT, tile_of(gres, u), ALU.mult).then_inc(s["b_zz"], 1)

            def b_ors(u):
                rsqrt(variance(omv), ove, ors, EPS_LN, "b_omv", Q * u + Q, "b_ove", "b_ors", u)

            def b_x1(u):
                pool.wait_ge(s["b_dd"], Q * u + Q)
                pool.tensor_tensor(tile_of(xres, u), tile_of(xres, u), dd, ALU.add).then_inc(s["b_x1"], 1)

            def b_xrs(u):
                rsqrt(variance(xmv), xve, xrs, EPS_LN, "b_xmv", Q * u + Q, "b_xve", "b_xrs", u)

            def f_rs(t):
                rsqrt(variance(fmv), fve, frs, EPS_LN, "f_mv", Q * t + Q, "f_ve", "f_rs", t)

            def f_out(t):
                pool.wait_ge(s["f_dd"], Q * t + Q)
                wait_past(pool, "out_done", 16 * t)
                pool.tensor_tensor(ob, tile_of(xres, t), dd2, ALU.add).then_inc(s["f_ob"], 1)

            def b_hi(t, g, j, par):
                n = J * g + j
                if j == 0:
                    pool.wait_ge(s["b_proj"], g + 1)
                wait_apart(pool, "b_gelu", n + 1)
                pool.tensor_scalar(hh[par][j], h32[j], H_SCALE, 0.0, ALU.mult, ALU.add).then_inc(s["b_hi"], 1)

            def b_piece(u, e):
                if e == 2:
                    b_gate(u)
                if e == 3:
                    b_ors(u)
                if e == 4:
                    b_x1(u)
                if e == 5:
                    b_xrs(u)

            def f_piece(t, e):
                if e == 1:
                    f_rs(t)
                if e == 2:
                    f_out(t)

            def b_tile(t, tp):
                for e in range(EXP):
                    for j in range(J):
                        b_hi(t, EXP * t + e, j, (EXP * tp + e) % 2)
                    if not is_int(t) or t + 1 < TILES:
                        b_piece(t + 1, e)
                    if not is_int(t) or t > 0:
                        f_piece(t - 1, e)
                    if not is_int(t) or t + 2 < TILES:
                        g_piece(t + 2, e, tp)

            pool.wait_ge(s["const"], 7)
            a_rstd(0, 0)
            pool.wait_ge(s["xt0_zero"], 1)
            a_rstd(1, 1)
            a_shift(0, 0, 0)
            a_ruk(0, 0)
            a_tile(0, 0)
            a_tile(0, 1)
            with pool.Fori(1, PAIRS - 1) as i:
                a_tile(i, 0)
                a_tile(i, 1)
            a_tile(PAIRS - 1, 0)
            a_tile(PAIRS - 1, 1)

            for e in range(EXP):
                b_piece(0, e)
            for e in range(EXP):
                g_piece(1, e, 1)
            b_tile(0, 0)
            b_tile(1, 1)
            with pool.Fori(1, PAIRS - 1) as i:
                b_tile(2 * i, 0)
                b_tile(2 * i + 1, 1)
            b_tile(TILES - 2, 0)
            b_tile(TILES - 1, 1)
            for e in range(EXP):
                f_piece(TILES - 1, e)

        @block.scalar
        def _(act):
            def copy(o, i):
                return act.activation(o, i, ACT.Copy)

            act.wait_ge(s["decay_ps"], 1)
            act.activation(dexp[:, 0:1], bkV[0][:, 0:1], ACT.Exp).then_inc(s["decay_e"], 1)
            copy(ucol[:, :], bkV[0][:, 1:2]).then_inc(s["decay_r"], 1)
            act.wait_ge(s["decay_e"], 1)
            act.activation(wcol[:, :], dexp[:, 0:1], ACT.Exp, scale=-1.0).then_inc(s["decay_r"], 1)
            for n in range(5):
                act.wait_ge(s["setup_t"], n + 1)
                copy(wt[:, n, :], bank[n % 4][:, 0:C]).then_inc(s["setup_ev"], 1)
            act.wait_ge(s["setup_t"], 6)
            copy(pcol[:, :], bkV[1][:, 0:NB]).then_inc(s["setup_ev"], 1)
            act.activation(bps[:, :], bprow[:, :], ACT.Copy, scale=1.0 / PROJ_DESCALE).then_inc(s["setup_ev"], 1)
            act.activation(wrt_hi[:, :], wrt[:, :], ACT.Copy, scale=W_SCALE).then_inc(s["setup_ev"], 1)

            def a_xT(t, par):
                act.wait_ge(s["a_xT_ps"], t + 1)
                copy(xT[par][:, 1:TOK + 1], bkA[:, :]).then_inc(s["a_xT"], 1)
                if par:
                    wait_past(act, "a_xT", t)
                    copy(xT[1][:, 0:1], xT[0][:, TOK:TOK + 1]).then_inc(s["a_edge"], 1)

            def a_xn(t):
                wait_past(act, "a_xT_ps", t)
                act.wait_ge(s["a_nmr"], t + 1)
                for q in range(Q):
                    act.activation(xn[:, q * P:(q + 1) * P], chunk_of(xres, t, q), ACT.Identity,
                                   bias=anmr[:, q:q + 1], scale=ars[:, q:q + 1]).then_inc(s["a_xn"], 1)

            def split(i):
                if i == 0:
                    act.wait_ge(s["wexp_in"], 16 * 2 * EXP)
                else:
                    act.wait_ge(s["split_lo"], i)
                act.activation(w_hi(i), w_stage(i), ACT.Copy, scale=W_SCALE).then_inc(s["split_hi"], 1)

            def a_k(t, par):
                act.wait_ge(s["a_k_ps"], t + 1)
                copy(kch[par], bkC[:, :]).then_inc(s["a_k"], 1)
                wait_past(act, "a_ruk", t)
                act.activation(uk, bkC[:, :], ACT.Copy, scale=ucol[:, 0:1]).then_inc(s["a_uk"], 1)

            def a_r(t, par):
                act.wait_ge(s["a_r_ps"], t + 1)
                copy(rch[par], bkB[:, :]).then_inc(s["a_r"], 1)

            def a_g(t):
                act.wait_ge(s["a_g_ps"], t + 1)
                act.activation(tile_of(gres, t), bkD[:, :], ACT.Gelu).then_inc(s["a_g"], 1)

            def a_rk(t):
                act.wait_ge(s["a_rk_ps"], t + 1)
                wait_past(act, "a_yu", t)
                copy(rk, bkB[:, 0:Q * H]).then_inc(s["a_rk"], 1)

            def a_yev(t, b):
                act.wait_ge(s["a_sel"], N * t + N // 2 * (b + 1) + RS)
                copy(ych[b], bkY[b][:, :]).then_inc(s["a_yev"], 1)

            def a_tile(t, par, first, last, ending):
                if not last:
                    a_xT(t + 1, 1 - par)
                else:
                    g_piece(0, 1)
                a_rk(t)
                if not first:
                    a_yev(t - 1, 1)
                if t == TILES - 2 if is_int(t) else False:
                    split(0)
                if last:
                    split(1)
                    split(2)
                a_yev(t, 0)
                if last:
                    split(3)
                if not last:
                    a_k(t + 1, 1 - par)
                if not ending:
                    a_xn(t + 2)
                if not last:
                    a_r(t + 1, 1 - par)
                    a_g(t + 1)

            def g_piece(u, e):
                if e == 1:
                    act.wait_ge(s["g_yc"], u + 1)
                    act.activation(sq, yc, ACT.Square).then_inc(s["g_sq"], 1)

            def b_piece(u, e, up):
                if e == 1:
                    act.wait_ge(s["b_ynT"], u + 1)
                    act.activation(zT, bkX[:, :], ACT.Identity, bias=pcol[:, LN_B:LN_B + 1],
                                   scale=pcol[:, LN_W:LN_W + 1]).then_inc(s["b_zT"], 1)
                if e == 6:
                    act.wait_ge(s["b_xn2T"], u + 1)
                    act.activation(xh[up], bkX[:, :], ACT.Copy, scale=X_SCALE).then_inc(s["b_xh"], 1)
                if e == 8:
                    act.wait_ge(s["b_lgd"], u + 1)
                    act.activation(ex, lg, ACT.Exp, scale=FC_DESCALE).then_inc(s["b_ex"], 1)

            def b_g9(u):
                act.wait_ge(s["b_gT"], u + 1)
                copy(g9, bkX[0:EXP, :]).then_inc(s["b_g9"], 1)

            def b_bias(u, up):
                wait_past(act, "f_dd", Q * (u - 1))
                act.wait_ge(s["b_bias"], u + 1)
                copy(acc[up], bkZ[:, :]).then_inc(s["b_acc"], 1)

            def b_gelu(g, e, j):
                n = J * g + j
                act.wait_ge(s["b_fc"], n + 1)
                act.wait_ge(s["b_lo"], n + 1)
                act.activation(h32[j], bkF[j][:, :], ACT.Gelu_apprx_tanh, bias=pcol[:, e * J + j:e * J + j + 1],
                               scale=FC_DESCALE).then_inc(s["b_gelu"], 1)

            def b_tile(t, tp):
                for e in range(EXP):
                    for j in range(J):
                        b_gelu(EXP * t + e, e, j)
                    if e == 0:
                        b_g9(t)
                        b_bias(t, tp)
                    if is_int(t) and t == 0:
                        for i in chunks_at(e):
                            split(i)
                    if not is_int(t) or t + 1 < TILES:
                        b_piece(t + 1, e, 1 - tp)
                    if not is_int(t) or t + 2 < TILES:
                        g_piece(t + 2, e)

            a_xn(0)
            act.wait_ge(s["setup_ev"], 8)
            a_xT(0, 0)
            a_k(0, 0)
            a_r(0, 0)
            a_g(0)
            a_xn(1)
            a_tile(0, 0, True, False, False)
            a_tile(1, 1, False, False, False)
            with act.Fori(1, PAIRS - 1) as i:
                a_tile(2 * i, 0, False, False, False)
                a_tile(2 * i + 1, 1, False, False, False)
            a_tile(TILES - 2, 0, False, False, True)
            a_tile(TILES - 1, 1, False, True, True)
            for i in range(4, 7):
                split(i)
            b_piece(0, 1, 0)
            a_yev(TILES - 1, 1)
            for i in range(7, 10):
                split(i)
            g_piece(1, 1)
            b_piece(0, 6, 0)
            split(10)
            b_piece(0, 8, 0)
            split(11)
            b_tile(0, 0)
            b_tile(1, 1)
            with act.Fori(1, PAIRS - 1) as i:
                b_tile(2 * i, 0)
                b_tile(2 * i + 1, 1)
            b_tile(TILES - 2, 0)
            b_tile(TILES - 1, 1)

        @block.vector
        def _(dve):
            def sub_scale(o, i, mean, rstd):
                return dve.tensor_scalar(o, i, mean, rstd, ALU.subtract, ALU.mult)

            dve.memset(xT[0][:, 0:1], 0.0).then_inc(s["xt0_zero"], 1)
            dve.memset(kv[0][:, 0:1], 0.0).then_inc(s["a_sel"], RS)
            dve.memset(kv[0][:, 1:2], 0.0).then_inc(s["b_lo"], J)
            dve.memset(kv[0][:, 2:3], 0.0).then_inc(s["b_proj"], 2)
            dve.memset(kv[0][:, 3:4], 0.0).then_inc(s["b_comb"], 2 * Q)

            def a_stats(t, par):
                wait_past(dve, "a_mv", Q * t)
                for q in range(Q):
                    dve.bn_stats(ast[:, 6 * q:6 * q + 6], chunk_of(xres, t, q)).then_inc(s["a_stats"], 1)

            def a_moments(t, par):
                wait_past(dve, "a_nmr", t - 1)
                wait_apart(dve, "a_stats", Q * t + Q)
                for q in range(Q):
                    dve.bn_aggr(amv[par][:, 2 * q:2 * q + 2], ast[:, 6 * q:6 * q + 6]).then_inc(s["a_mv"], 1)

            def a_mix(t, par, n, col):
                if n == 0:
                    dve.wait_ge(s["a_xx"], t + 1)
                if n:
                    wait_past(dve, ("a_k_ps", "a_r_ps", "a_g_ps")[n - 1], t)
                dve.scalar_tensor_tensor(out=(xmix_v[par], xmix_k, xmix_r, xmix_g)[n], in0=xx, scalar=pcol[:, col:col + 1],
                                         in1=xT[par][:, 1:TOK + 1], op0=ALU.mult, op1=ALU.add).then_inc(s["a_mix"], 1)

            MIX = (MAA_V, MAA_K, MAA_R, MAA_G)
            MIX_AT = (2, 3, 5, 6)

            def a_kv(t, par, m):
                n = N * t + m
                dve.wait_ge(s["a_vrep"], n + 1)
                if m == 0:
                    dve.wait_ge(s["a_k"], t + 1)
                dve.tensor_tensor(kv[m % 2], bkV[m % 2][:, :], kch[par], ALU.mult).then_inc(s["a_kv"], 1)
                if par:
                    dve.wait_ge(s["a_rs"], n - N + 1)
                    dve.tensor_copy(S[m][:, 0:1], S[m][:, TOK:TOK + 1]).then_inc(s["a_carry"], 1)
                else:
                    wait_past(dve, "a_rs", n - N + 1)
                    dve.memset(S[m][:, 0:1], 0.0).then_inc(s["a_carry"], 1)

            def a_scan(t, m):
                n = N * t + m
                dve.wait_ge(s["a_kv"], n + 1)
                dve.wait_ge(s["a_carry"], n + 1)
                dve.tensor_tensor_scan(S[m][:, 1:TOK + 1], wcol[:, 0:1].to_broadcast([P, TOK]), kv[m % 2],
                                       S[m][:, 0:1], ALU.mult, ALU.add).then_inc(s["a_scan"], 1)

            def split(i):
                dve.wait_ge(s["split_hi"], i + 1)
                dve.scalar_tensor_tensor(out=w_lo(i), in0=w_stage(i), scalar=W_SCALE, in1=w_hi(i),
                                         op0=ALU.mult, op1=ALU.subtract).then_inc(s["split_lo"], 1)

            def a_yu(t):
                dve.wait_ge(s["a_vt"], t + 1)
                dve.wait_ge(s["a_rk"], t + 1)
                dve.tensor_tensor(tile_of(yres, t).rearrange("p (h m) -> p h m", m=N),
                                  bkA[:, :].rearrange("p (h m) -> p h m", m=N),
                                  rk.unsqueeze(2).to_broadcast([P, Q * H, N]), ALU.mult).then_inc(s["a_yu"], 1)

            def a_y(t):
                dve.wait_ge(s["a_yu"], t + 1)
                for b in range(2):
                    dve.wait_ge(s["a_yT"], 2 * t + b + 1)
                    y = tile_of(yres, t).rearrange("p (q h b g) -> p q h b g", h=H, b=2, g=4)[:, :, :, b, :]
                    ps = (bkC, bkD)[b][:, :].rearrange("p (q g h) -> p q h g", g=4, h=32)[:, :, 0:H, :]
                    dve.tensor_tensor(y, ps, y, ALU.add).then_inc(s["a_y"], 1)

            def a_tile(t, par):
                first, last, ending = (is_int(t) and v for v in (t == 0, t == TILES - 1, t >= TILES - 2))
                for m in range(N):
                    a_kv(t, par, m)
                    if m == 0 and not ending:
                        if is_int(t) and t == 0:
                            dve.wait_ge(s["x_second_in"], 16)
                        a_stats(t + 2, par)
                    if m == 1 and not ending:
                        a_moments(t + 2, par)
                    if m in MIX_AT and not last:
                        n = MIX_AT.index(m)
                        a_mix(t + 1, 1 - par, n, MIX[n])
                    if m == 4 and not first:
                        a_y(t - 1)
                    if m == 4 and ending and not last:
                        split(0)
                    if last:
                        if m % 2 == 0:
                            g_piece(0, m // 2)
                        if m in (3, 5, 6):
                            split(m - 2 if m == 3 else m - 3)
                    if m == 7:
                        a_yu(t)
                    a_scan(t, m)

            def stats(src, st, mv, s_st, s_mv, t):
                for q in range(Q):
                    dve.bn_stats(st[:, 6 * q:6 * q + 6], src(q)).then_inc(s[s_st], 1)
                wait_apart(dve, s_st, Q * t + Q)
                for q in range(Q):
                    dve.bn_aggr(mv[:, 2 * q:2 * q + 2], st[:, 6 * q:6 * q + 6]).then_inc(s[s_mv], 1)

            def normalise(dst, src, mv, rs, s_out):
                for q in range(Q):
                    sub_scale(dst[:, q * P:(q + 1) * P], src(q), mv[:, 2 * q:2 * q + 1],
                              rs[:, q:q + 1]).then_inc(s[s_out], 1)

            def per_expert(a):
                return a.rearrange("p (q e) -> p q e", e=E)

            def over_experts(a):
                return a.unsqueeze(2).to_broadcast([P, Q, E])

            def g_piece(u, e):
                y3 = tile_of(yres, u).rearrange("p (h m) -> p h m", m=N)
                if e == 0:
                    dve.tensor_reduce(s64, y3, AX.X, ALU.add).then_inc(s["g_s"], 1)
                    wait_past(dve, "g_yn", u)
                    dve.wait_ge(s["g_s"], u + 1)
                    dve.scalar_tensor_tensor(out=yc.rearrange("p (h m) -> p h m", m=N),
                                             in0=s64.unsqueeze(2).to_broadcast([P, Q * H, N]), scalar=-1.0 / N,
                                             in1=y3, op0=ALU.mult, op1=ALU.add).then_inc(s["g_yc"], 1)
                if e == 1:
                    dve.wait_ge(s["g_sq"], u + 1)
                    dve.tensor_reduce(v64, sq.rearrange("p (h m) -> p h m", m=N), AX.X, ALU.add).then_inc(s["g_v"], 1)
                if e == 2:
                    dve.wait_ge(s["g_ve"], u + 1)
                    dve.tensor_scalar(gshift, gve.bitcast(U32), 1, None, ALU.logical_shift_right)\
                       .then_inc(s["g_shift"], 1)
                    dve.wait_ge(s["g_shift"], u + 1)
                    dve.tensor_scalar(grs.bitcast(U32), gshift, -1.0, float(GUESS), ALU.mult, ALU.add)\
                       .then_inc(s["g_guess"], 1)

            def b_piece(u, e, up):
                if e == 2:
                    dve.wait_ge(s["b_o"], u + 1)
                    stats(lambda q: bkZ[:, q * P:(q + 1) * P], ost, omv, "b_ost", "b_omv", u)
                if e == 3:
                    dve.wait_ge(s["b_ors"], u + 1)
                    normalise(dd, lambda q: bkZ[:, q * P:(q + 1) * P], omv, ors, "b_dd")
                if e == 4:
                    dve.wait_ge(s["b_x1"], u + 1)
                    stats(lambda q: chunk_of(xres, u, q), xst, xmv, "b_xst", "b_xmv", u)
                if e == 5:
                    dve.wait_ge(s["b_xrs"], u + 1)
                    normalise(xn2, lambda q: chunk_of(xres, u, q), xmv, xrs, "b_xn2")
                if e == 6:
                    dve.wait_ge(s["b_xh"], u + 1)
                    dve.scalar_tensor_tensor(out=xl[up], in0=bkX[:, :], scalar=X_SCALE, in1=xh[up],
                                             op0=ALU.mult, op1=ALU.subtract).then_inc(s["b_xl"], 1)
                if e == 7:
                    dve.wait_ge(s["b_lg"], u + 1)
                    z3 = bkZ[:, 0:Q * E].rearrange("p (q e) -> p q e", e=E)
                    dve.tensor_reduce(mx, z3, AX.X, ALU.max).then_inc(s["b_mx"], 1)
                    dve.wait_ge(s["b_mx"], u + 1)
                    dve.tensor_tensor(per_expert(lg), z3, over_experts(mx), ALU.subtract).then_inc(s["b_lgd"], 1)
                if e == 8:
                    dve.wait_ge(s["b_ex"], u + 1)
                    dve.tensor_reduce(se, per_expert(ex), AX.X, ALU.add).then_inc(s["b_se"], 1)
                    dve.wait_ge(s["b_se"], u + 1)
                    dve.reciprocal(rse, se).then_inc(s["b_rse"], 1)
                    dve.wait_ge(s["b_rse"], u + 1)
                    dve.tensor_tensor(per_expert(pr), per_expert(ex), over_experts(rse), ALU.mult)\
                       .then_inc(s["b_pr"], 1)
                    wait_apart(dve, "b_pr", u + 1)
                    for q in range(Q):
                        dve.max(top[:, 8 * q:8 * q + 8], pr[:, E * q:E * q + E]).then_inc(s["b_top"], 1)
                    wait_apart(dve, "b_top", Q * u + Q)
                    for q in range(Q):
                        dve.max_index(tix[:, 8 * q:8 * q + 8], top[:, 8 * q:8 * q + 8], pr[:, E * q:E * q + E])\
                           .then_inc(s["b_tix"], 1)
                    top3 = top.rearrange("p (q k) -> p q k", k=8)
                    dve.tensor_tensor(s2.unsqueeze(2), top3[:, :, 0:1], top3[:, :, 1:2], ALU.add)\
                       .then_inc(s["b_s2"], 1)
                    dve.wait_ge(s["b_s2"], u + 1)
                    dve.reciprocal(r2, s2).then_inc(s["b_r2"], 1)
                    dve.wait_ge(s["b_tix"], Q * u + Q)
                    dve.tensor_copy(tif, tix).then_inc(s["b_eq"], 1)
                    dve.wait_ge(s["b_r2"], u + 1)
                    g23 = g2.rearrange("p (q k) -> p q k", k=2)
                    dve.scalar_tensor_tensor(out=g23, in0=top3[:, :, 0:2], scalar=PROJ_DESCALE,
                                             in1=r2.unsqueeze(2).to_broadcast([P, Q, 2]), op0=ALU.mult,
                                             op1=ALU.mult).then_inc(s["b_g2"], 1)
                    dve.wait_ge(s["b_eq"], 5 * u + 1)
                    tif3 = tif.rearrange("p (q k) -> p q k", k=8)
                    io = iota8[:, :].unsqueeze(1).to_broadcast([P, Q, E])
                    for k in range(2):
                        dve.tensor_tensor(per_expert(eq[k]), io, tif3[:, :, k:k + 1].to_broadcast([P, Q, E]),
                                          ALU.is_equal).then_inc(s["b_eq"], 1)
                    dve.wait_ge(s["b_g2"], u + 1)
                    for k in range(2):
                        dve.wait_ge(s["b_eq"], 5 * u + 2 + k)
                        dve.tensor_tensor(per_expert(eq[k]), per_expert(eq[k]),
                                          g23[:, :, k:k + 1].to_broadcast([P, Q, E]), ALU.mult)\
                           .then_inc(s["b_eq"], 1)
                    dve.wait_ge(s["b_eq"], 5 * u + 5)
                    dve.tensor_tensor(gates[up][:, :, 0:E], per_expert(eq[0]), per_expert(eq[1]), ALU.add)\
                       .then_inc(s["b_gate"], 1)

            def b_lo(g, j, par):
                n = J * g + j
                dve.wait_ge(s["b_hi"], n + 1)
                dve.scalar_tensor_tensor(out=hl[par][j], in0=h32[j], scalar=H_SCALE, in1=hh[par][j],
                                         op0=ALU.mult, op1=ALU.subtract).then_inc(s["b_lo"], 1)

            def b_comb(t, g, e, tp, par):
                dve.wait_ge(s["b_proj"], g + 1 + 2)
                if e == 0:
                    dve.wait_ge(s["b_acc"], t + 1)
                for q in range(Q):
                    a = acc[tp][:, q * P:(q + 1) * P]
                    dve.wait_ge(s["b_comb"], Q * g + q + 1 - Q + 2 * Q)
                    dve.scalar_tensor_tensor(out=a, in0=bkP[par][:, q * P:(q + 1) * P],
                                             scalar=gates[tp][:, q, e:e + 1], in1=a,
                                             op0=ALU.mult, op1=ALU.add).then_inc(s["b_comb"], 1)

            def f_stats(t, tp):
                dve.wait_ge(s["b_comb"], Q * EXP * (t + 1) + 2 * Q)
                stats(lambda q: acc[tp][:, q * P:(q + 1) * P], fst, fmv, "f_st", "f_mv", t)

            def f_norm(t, tp):
                dve.wait_ge(s["f_rs"], t + 1)
                wait_past(dve, "f_ob", t)
                normalise(dd2, lambda q: acc[tp][:, q * P:(q + 1) * P], fmv, frs, "f_dd")

            def b_tile(t, tp):
                for e in range(EXP):
                    g = EXP * t + e
                    par = (EXP * tp + e) % 2
                    for j in range(J):
                        b_lo(g, j, par)
                    if e:
                        b_comb(t, g - 1, e - 1, tp, 1 - par)
                    if is_int(t) and t == 0:
                        for i in chunks_at(e):
                            split(i)
                    if not is_int(t) or t > 0:
                        if e == 0:
                            b_comb(t - 1, g - 1, EXP - 1, 1 - tp, 1 - par)
                            f_stats(t - 1, 1 - tp)
                        if e == 1:
                            f_norm(t - 1, 1 - tp)
                    if not is_int(t) or t + 1 < TILES:
                        b_piece(t + 1, e, 1 - tp)
                    if not is_int(t) or t + 2 < TILES:
                        g_piece(t + 2, e)

            dve.wait_ge(s["x_first_in"], 16)
            a_stats(0, 0)
            a_moments(0, 0)
            a_stats(1, 1)
            a_moments(1, 1)
            dve.wait_ge(s["setup_ev"], 8)
            for m in range(N):
                src = wt[:, V_, :].rearrange("p (h m) -> p h m", m=N)[:, :, m:m + 1].to_broadcast([P, H, N])
                dve.tensor_copy(wvrep[:, m, :].rearrange("p (h n) -> p h n", n=N), src).then_inc(s["wvrep_done"], 1)
            dve.scalar_tensor_tensor(out=wrt_lo[:, :], in0=wrt[:, :], scalar=W_SCALE, in1=wrt_hi[:, :],
                                     op0=ALU.mult, op1=ALU.subtract).then_inc(s["wvrep_done"], 1)
            for n in range(4):
                a_mix(0, 0, n, MIX[n])
            dve.wait_ge(s["decay_r"], 2)
            a_tile(0, 0)
            a_tile(1, 1)
            dve.wait_ge(s["x_rest_in"], 16 * (B - 2))
            with dve.Fori(1, PAIRS - 1) as i:
                a_tile(2 * i, 0)
                a_tile(2 * i + 1, 1)
            a_tile(TILES - 2, 0)
            a_tile(TILES - 1, 1)
            for i in range(4, 7):
                split(i)
            b_piece(0, 2, 0)
            split(7)
            b_piece(0, 3, 0)
            a_y(TILES - 1)
            b_piece(0, 4, 0)
            split(8)
            b_piece(0, 5, 0)
            split(9)
            g_piece(1, 0)
            b_piece(0, 6, 0)
            b_piece(0, 7, 0)
            split(10)
            g_piece(1, 1)
            g_piece(1, 2)
            b_piece(0, 8, 0)
            split(11)
            b_tile(0, 0)
            b_tile(1, 1)
            with dve.Fori(1, PAIRS - 1) as i:
                b_tile(2 * i, 0)
                b_tile(2 * i + 1, 1)
            b_tile(TILES - 2, 0)
            b_tile(TILES - 1, 1)
            b_comb(TILES - 1, EXP * TILES - 1, EXP - 1, 1, (EXP * TILES - 1) % 2)
            f_stats(TILES - 1, 1)
            f_norm(TILES - 1, 1)

        @block.tensor
        def _(pe):
            def mm(o, lhsT, rhs, start=True, stop=True, **k):
                return pe.matmul(o, lhsT, rhs, start=start, stop=stop, **k)

            pe.wait_ge(s["const"], 7)
            pe.wait_ge(s["params_in"], N_PARAMS)
            mm(bkV[0][:, 0:2], selT[:, :], dcol[:, :]).then_inc(s["decay_ps"], 1)
            for n in range(5):
                if n >= 4:
                    pe.wait_ge(s["setup_ev"], n - 3)
                pe.transpose(bank[n % 4][:, 0:C], wraw[n], ident[:, :]).then_inc(s["setup_t"], 1)
            pe.transpose(bkV[1][:, 0:NB], prow, ident[0:NB, 0:NB]).then_inc(s["setup_t"], 1)

            def a_T(t):
                pe.wait_ge(s["a_xn"], Q * t + Q)
                wait_past(pe, "a_yu", t - 1)
                for q in range(Q):
                    i = pe.transpose(bkA[:, q * P:(q + 1) * P], xn[:, q * P:(q + 1) * P], ident[:, :])
                i.then_inc(s["a_xT_ps"], 1)

            def a_k(t):
                pe.wait_ge(s["a_mix"], 4 * t + 2)
                wait_past(pe, "a_y", 2 * t - 2)
                mm(bkC[:, :], wt[:, K_, :], xmix_k).then_inc(s["a_k_ps"], 1)

            def a_r(t):
                pe.wait_ge(s["a_mix"], 4 * t + 3)
                wait_past(pe, "a_rk", t)
                mm(bkB[:, :], wt[:, R_, :], xmix_r).then_inc(s["a_r_ps"], 1)

            def a_g(t):
                pe.wait_ge(s["a_mix"], 4 * t + 4)
                mm(bkD[:, :], wt[:, G_, :], xmix_g).then_inc(s["a_g_ps"], 1)

            def a_vrep(t, par, m, lead):
                if not lead:
                    pe.wait_ge(s["a_kv"], N * t + m - 1)
                mm(bkV[m % 2][:, :], wvrep[:, m, :], xmix_v[par]).then_inc(s["a_vrep"], 1)

            def a_sel(t, m):
                if m % 4 == 0:
                    wait_past(pe, "a_yev", 2 * t - 1 + m // 4)
                pe.wait_ge(s["a_rs"], N * t + m + 1)
                g = 32 * (m % 4)
                mm(bkY[m // 4][g:g + 32, :], sel[:, :], rS[m % RS]).then_inc(s["a_sel"], 1)

            def a_vtok(t, par, last):
                pe.wait_ge(s["a_xT"], t + 1 if last else t + 2)
                for q in range(Q):
                    i = mm(bkA[:, q * P:(q + 1) * P], xmix_v[par][:, q * P:(q + 1) * P], wt[:, V_, :])
                i.then_inc(s["a_vt"], 1)

            def a_rk(t):
                pe.wait_ge(s["a_ruk"], t + 1)
                for q in range(Q):
                    i = mm(bkB[:, q * H:(q + 1) * H], ruk[:, q * P:(q + 1) * P], sel[:, 0:H])
                i.then_inc(s["a_rk_ps"], 1)

            def a_yT(t):
                for b in range(2):
                    pe.wait_ge(s["a_yev"], 2 * t + b + 1)
                    if not is_int(t) or t + 1 < TILES:
                        pe.wait_ge(s["a_g" if b else "a_uk"], t + 2)
                    for q in range(Q):
                        i = pe.transpose((bkC, bkD)[b][:, q * P:(q + 1) * P], ych[b][:, q * P:(q + 1) * P],
                                         ident[:, :])
                    i.then_inc(s["a_yT"], 1)

            def a_tile(t, par, first, last):
                for m in range(N):
                    if m == 0 and not last:
                        a_T(t + 1)
                    if m + 2 < N:
                        a_vrep(t, par, m + 2, False)
                    elif not last:
                        a_vrep(t + 1, 1 - par, m + 2 - N, False)
                    if m >= 2:
                        a_sel(t, m - 2)
                    elif not first:
                        a_sel(t - 1, m + N - 2)
                    if m == 1:
                        a_rk(t)
                    if m == 2 and not first:
                        a_yT(t - 1)
                    if m == 3:
                        a_vtok(t, par, last)
                    if m == 5 and not last:
                        a_k(t + 1)
                    if m == 6 and not last:
                        a_r(t + 1)
                    if m == 7 and not last:
                        a_g(t + 1)

            def b_piece(u, e, up):
                if e == 1:
                    wait_past(pe, "b_g9", u)
                    pe.wait_ge(s["g_yn"], u + 1)
                    for q in range(Q):
                        i = pe.transpose(bkX[:, q * P:(q + 1) * P], yn[up][:, q * P:(q + 1) * P], ident[:, :])
                    i.then_inc(s["b_ynT"], 1)
                if e == 2:
                    wait_past(pe, "b_acc", u)
                    pe.wait_ge(s["b_zz"], u + 1)
                    for q in range(Q):
                        i = mm(bkZ[:, q * P:(q + 1) * P], zz[:, q * P:(q + 1) * P], wt[:, O_, :])
                    i.then_inc(s["b_o"], 1)
                if e == 6:
                    pe.wait_ge(s["b_xn2"], Q * u + Q)
                    for q in range(Q):
                        i = pe.transpose(bkX[:, q * P:(q + 1) * P], xn2[:, q * P:(q + 1) * P], ident[:, :])
                    i.then_inc(s["b_xn2T"], 1)
                if e == 7:
                    pe.wait_ge(s["b_xl"], u + 1)
                    for q in range(Q):
                        xs = slice(q * P, (q + 1) * P)
                        o = bkZ[:, q * E:(q + 1) * E]
                        mm(o, xh[up][:, xs], wrt_lo[:, :], True, False)
                        mm(o, xl[up][:, xs], wrt_hi[:, :], False, False)
                        i = mm(o, xh[up][:, xs], wrt_hi[:, :], False, True)
                    i.then_inc(s["b_lg"], 1)

            def b_gT(u, up):
                pe.wait_ge(s["b_gate"], u + 1)
                for q in range(Q):
                    i = pe.transpose(bkX[0:EXP, q * P:(q + 1) * P], gates[up][:, q, :], ident[:, :])
                i.then_inc(s["b_gT"], 1)

            def b_bias(u):
                pe.wait_ge(s["b_g9"], u + 1)
                for q in range(Q):
                    i = mm(bkZ[:, q * P:(q + 1) * P], g9[:, q * P:(q + 1) * P], bps[:, :])
                i.then_inc(s["b_bias"], 1)

            def b_fc(g, e, up, lead):
                if is_int(g) and g < EXP:
                    pe.wait_ge(s["split_lo"], fc(e) + 1)
                for j in range(J):
                    if not lead:
                        pe.wait_ge(s["b_gelu"], J * (g - 1) + j + 1)
                    js = slice(j * P, (j + 1) * P)
                    mm(bkF[j][:, :], w_lo(fc(e))[:, js], xh[up], True, False)
                    mm(bkF[j][:, :], w_hi(fc(e))[:, js], xl[up], False, False)
                    mm(bkF[j][:, :], w_hi(fc(e))[:, js], xh[up], False, True).then_inc(s["b_fc"], 1)

            def b_proj(g, e, par):
                if is_int(g) and g < EXP:
                    pe.wait_ge(s["split_lo"], proj(e) + 1)
                pe.wait_ge(s["b_lo"], J * (g + 1) + J)
                pe.wait_ge(s["b_comb"], Q * (g + 1))
                for q in range(Q):
                    o = bkP[par][:, q * P:(q + 1) * P]
                    qs = slice(q * P, (q + 1) * P)
                    for j in range(J):
                        js = slice(j * P, (j + 1) * P)
                        mm(o, hl[par][j][:, qs], w_hi(proj(e))[:, js], j == 0, False)
                        mm(o, hh[par][j][:, qs], w_lo(proj(e))[:, js], False, False)
                        i = mm(o, hh[par][j][:, qs], w_hi(proj(e))[:, js], False, j == J - 1)
                i.then_inc(s["b_proj"], 1)

            def b_tile(t, tp):
                last = is_int(t) and t + 1 == TILES
                for e in range(EXP):
                    g = EXP * t + e
                    if not last:
                        b_piece(t + 1, e, 1 - tp)
                    if e == 0:
                        b_gT(t, tp)
                    if e + 1 < EXP:
                        b_fc(g + 1, e + 1, tp, False)
                    elif not last:
                        b_fc(g + 1, 0, 1 - tp, False)
                    if e == 0:
                        b_bias(t)
                    b_proj(g, e, (EXP * tp + e) % 2)

            pe.wait_ge(s["setup_ev"], 8)
            pe.wait_ge(s["decay_r"], 2)
            a_T(0)
            a_k(0)
            a_r(0)
            a_g(0)
            pe.wait_ge(s["wvrep_done"], N + 1)
            a_vrep(0, 0, 0, True)
            a_vrep(0, 0, 1, True)
            a_tile(0, 0, True, False)
            a_tile(1, 1, False, False)
            with pe.Fori(1, PAIRS - 1) as i:
                a_tile(2 * i, 0, False, False)
                a_tile(2 * i + 1, 1, False, False)
            a_tile(TILES - 2, 0, False, False)
            a_tile(TILES - 1, 1, False, True)
            pe.wait_ge(s["a_rk"], TILES)
            b_piece(0, 1, 0)
            a_sel(TILES - 1, N - 2)
            a_sel(TILES - 1, N - 1)
            pe.wait_ge(s["a_yu"], TILES)
            b_piece(0, 2, 0)
            a_yT(TILES - 1)
            b_piece(0, 6, 0)
            pe.wait_ge(s["a_y"], 2 * TILES)
            b_piece(0, 7, 0)
            b_fc(0, 0, 0, True)
            b_tile(0, 0)
            b_tile(1, 1)
            with pe.Fori(1, PAIRS - 1) as i:
                b_tile(2 * i, 0)
                b_tile(2 * i + 1, 1)
            b_tile(TILES - 2, 0)
            b_tile(TILES - 1, 1)


_INS = ['L0_attn_x', 'L0_attn_time_maa_k', 'L0_attn_time_maa_v', 'L0_attn_time_maa_r', 'L0_attn_time_maa_g',
        'L0_attn_time_decay', 'L0_attn_time_faaaa', 'L0_attn_Wr', 'L0_attn_Wk', 'L0_attn_Wv', 'L0_attn_Wg',
        'L0_attn_Wo', 'L0_attn_ln_w', 'L0_attn_ln_b', 'L0_ffn_Wfc_s', 'L0_ffn_bfc_s', 'L0_ffn_Wproj_s',
        'L0_ffn_bproj_s', 'L0_ffn_Wr', 'L0_ffn_Wfc', 'L0_ffn_bfc', 'L0_ffn_Wproj', 'L0_ffn_bproj']
_OUT = (8, 1024, 128)


def kernel(**inputs):
    import numpy as _np
    import concourse.bacc as _bacc
    from concourse.bass_utils import run_bass_kernel_spmd as _run

    nc = _bacc.Bacc("TRN2", target_bir_lowering=False, num_devices=1)
    arrays, args = {}, []
    for name in _INS:
        a = _np.ascontiguousarray(inputs[name])
        arrays[f"in_{name}"] = a
        args.append(nc.dram_tensor(f"in_{name}", a.shape, mybir.dt.from_np(a.dtype), kind="ExternalInput").ap())
    args.append(nc.dram_tensor("out_0", _OUT, F32, kind="ExternalOutput").ap())
    build(nc, *args)
    r = _run(nc, [arrays], core_ids=[0])
    return r.results[0]["out_0"]
```

```python
import concourse.bass as bass
from concourse import mybir
from contextlib import ExitStack

F32 = mybir.dt.float32
F16 = mybir.dt.float16
U32 = mybir.dt.uint32
ALU = mybir.AluOpType
ACT = mybir.ActivationFunctionType
AX = mybir.AxisListType

B, T, C = 8, 1024, 128
H, N = 16, 8
P = 128
TOK = 512
Q = TOK // P
TILES = B * T // TOK
PAIRS = TILES // 2
E = 8
EXP = E + 1
HID = 512
J = HID // P
EPS_LN = 1e-5
EPS_GN = 1e-5 * 64
W_SCALE = 2.0 ** 8
X_SCALE = 2.0 ** 8
H_SCALE = 2.0 ** 6
G_SCALE = 2.0 ** 8
FC_DESCALE = 1.0 / (W_SCALE * X_SCALE)
PROJ_DESCALE = 1.0 / (H_SCALE * W_SCALE)
BIAS_DESCALE = 1.0 / (G_SCALE * W_SCALE)
PG = 32
NEWTON = 3
GUESS = 0x5F3759DF
R_, K_, V_, G_, O_ = range(5)
MAA_K, MAA_V, MAA_R, MAA_G, LN_W, LN_B, BFC = range(7)
NB_MAA = MAA_G + 1
NB = BFC + EXP * J
RS = 4
SPLIT_AHEAD = 12
CH = 512


def is_int(t):
    return isinstance(t, int)


def build(nc, x, maa_k, maa_v, maa_r, maa_g, decay, faaaa, wr, wk, wv, wg, wo, ln_w, ln_b,
          wfc_s, bfc_s, wproj_s, bproj_s, w_router, wfc, bfc, wproj, bproj, out):
    ctx = ExitStack()
    with ctx:
        def sb(name, shape, dt=F32):
            return ctx.enter_context(nc.sbuf_tensor(name, shape, dt))

        def sem(name):
            return ctx.enter_context(nc.semaphore(name))

        xres = sb("xres", [P, TILES * TOK])
        yres = sb("yres", [P, TILES * TOK])
        gres = sb("gres", [P, TILES * TOK])
        wexp = sb("wexp", [P, (2 * EXP + 1) * CH])
        wt = sb("wt", [P, 5, C])
        wvrep = sb("wvrep", [P, N, P])
        ident = sb("ident", [P, P])
        sel = sb("sel", [P, 32])
        selT = sb("selT", [H, P])
        pcol = sb("pcol", [P, NB])
        wcol = sb("wcol", [P, 1])
        ucol = sb("ucol", [P, 1])
        neghalf = sb("neghalf", [P, Q])
        iota8 = sb("iota8", [P, E])
        wrt = sb("wrt", [P, E])
        wrt_hi = sb("wrt_hi", [P, E], F16)
        wrt_lo = sb("wrt_lo", [P, E], F16)
        bprow = sb("bprow", [3 * PG, C])
        bps = sb("bps", [3 * PG, C], F16)
        dcol = sb("dcol", [H, 2])
        gates = [sb(f"gates{i}", [P, Q, EXP]) for i in range(2)]

        WORK = 16400
        work = sb("work", [P, WORK])
        cut_at = [0]

        def cut(n, dt=F32):
            words = n if dt == F32 else n // 2
            a = cut_at[0]
            cut_at[0] += words
            assert cut_at[0] <= WORK, cut_at
            v = work[:, a:a + words]
            return v if dt == F32 else v.bitcast(dt)

        xn = cut(TOK)
        xT = [cut(TOK + 1) for _ in range(2)]
        cut_at[0] += cut_at[0] % 2
        xx = cut(TOK)
        xmix_k, xmix_r, xmix_g = (cut(TOK) for _ in range(3))
        xmix_v = [cut(TOK) for _ in range(2)]
        kch = [cut(TOK) for _ in range(2)]
        rch = [cut(TOK) for _ in range(2)]
        kv = [cut(TOK) for _ in range(2)]
        S_AT = cut_at[0]
        wraw = [cut(C) for _ in range(4)]
        prow_maa = cut(C)[0:NB_MAA, :]
        dexp = cut(2)
        cut_at[0] = S_AT
        S = [cut(TOK + 2) for _ in range(N)]
        rS = [cut(TOK) for _ in range(RS)]
        uk = cut(TOK)
        ruk = cut(TOK)
        woraw, prow_rest = (cut(C) for _ in range(2))
        prow_rest = prow_rest[0:NB - NB_MAA, :]
        cut_at[0] -= 2 * C
        ych = [cut(TOK) for _ in range(2)]
        rk = cut(Q * H)
        ast = cut(Q * 6)
        amv = [cut(Q * 2) for _ in range(2)]
        ave = cut(Q)
        ars = cut(Q)
        anm = cut(Q)
        anmr = cut(Q)
        cut_at[0] = 0
        s64 = cut(Q * H)
        v64 = cut(Q * H)
        gve = cut(Q * H)
        ghv = cut(Q * H)
        gshift = cut(Q * H).bitcast(U32)
        grs = cut(Q * H)
        gsq = cut(Q * H)
        gtm = cut(Q * H)
        gtf = cut(Q * H)
        yc = cut(TOK)
        sq = cut(TOK)
        yn = [cut(TOK) for _ in range(2)]
        zT = cut(TOK)
        zz = cut(TOK)
        dd = cut(TOK)
        xn2 = cut(TOK)
        xh = [cut(TOK, F16) for _ in range(2)]
        xl = [cut(TOK, F16) for _ in range(2)]
        h32 = [cut(TOK) for _ in range(J)]
        hh = [[cut(TOK, F16) for _ in range(J)] for _ in range(2)]
        hl = [[cut(TOK, F16) for _ in range(J)] for _ in range(2)]
        acc = [cut(TOK) for _ in range(2)]
        dd2 = cut(TOK)
        ob = cut(TOK)
        g3 = cut(Q * 3 * PG)
        g16 = cut(Q * EXP, F16)
        g3T = cut(TOK, F16)[0:3 * PG, :]
        ost = cut(Q * 6)
        omv = cut(Q * 2)
        ove = cut(Q)
        ors = cut(Q)
        xst = cut(Q * 6)
        xmv = cut(Q * 2)
        xve = cut(Q)
        xrs = cut(Q)
        fst = cut(Q * 6)
        fmv = cut(Q * 2)
        fve = cut(Q)
        frs = cut(Q)
        mx = cut(Q)
        lg = cut(Q * E)
        ex = cut(Q * E)
        se = cut(Q)
        rse = cut(Q)
        pr = cut(Q * E)
        top = cut(Q * 8)
        tix = cut(Q * 8).bitcast(U32)
        tif = cut(Q * 8)
        s2 = cut(Q)
        r2 = cut(Q)
        g2 = cut(Q * 2)
        eq = [cut(Q * E) for _ in range(2)]

        bank = [ctx.enter_context(nc.psum_tensor(f"bank{i}", [P, 512], F32)) for i in range(8)]

        s = {n: sem(n) for n in (
            "params_in other_params_in wexp_in x_first_in x_other_in x_second_in x_rest_in out_done "
            "const pool_set setup_t setup_ev late_t late_ev bias_zero g3_zero late_lo decay_ps decay_e decay_r "
            "wvrep_done xt0_zero split_hi split_lo "
            "a_stats a_mv a_ve a_rstd a_nm a_nmr a_xn a_xT_ps a_xT a_edge a_xx a_mix "
            "a_k_ps a_r_ps a_g_ps a_k a_uk a_r a_g "
            "a_vrep a_kv a_carry a_scan a_rs a_sel a_yev a_vt a_ruk a_rk_ps a_rk a_yu a_yT a_y "
            "g_s g_yc g_sq g_v g_ve g_hv g_shift g_guess g_newton g_yn "
            "b_ynT b_zT b_zz b_o b_ost b_omv b_ove b_ors b_dd b_x1 "
            "b_xst b_xmv b_xve b_xrs b_xn2 b_xn2T b_xh b_xl b_lg b_mx b_lgd b_ex b_se b_rse b_pr b_top b_tix "
            "b_s2 b_r2 b_g2 b_eq b_gate b_g16 b_g3 b_gT b_g3T b_bias b_acc "
            "b_fc b_gelu b_hi b_lo b_proj b_comb f_st f_mv f_ve f_rs f_dd f_ob").split()}

        bkA, bkB = bank[7], bank[6]
        bkC, bkD = bank[2:4]
        bkV, bkY = bank[4:6], bank[0:2]
        bkF, bkP, bkX, bkZ = bank[0:4], bank[4:6], bank[6], bank[7]

        def tile_of(res, t):
            return res[:, bass.ts(t, TOK)]

        def chunk_of(res, t, q):
            return res[:, bass.ds(t * TOK + q * P, P)]

        def fc(e):
            return 2 * e

        def proj(e):
            return 2 * e + 1

        def w_hi(i):
            return wexp[:, i * CH:i * CH + CH // 2].bitcast(F16)

        def w_lo(i):
            return wexp[:, i * CH + CH // 2:(i + 1) * CH].bitcast(F16)

        def w_stage(i):
            return wexp[:, (i + 1) * CH:(i + 2) * CH]

        def chunks_at(e):
            return range(SPLIT_AHEAD + e, min(SPLIT_AHEAD + e + 1, 2 * EXP))

        def wait_past(eng, name, value):
            if not isinstance(value, int) or value > 0:
                eng.wait_ge(s[name], value)

        def wait_apart(eng, name, value):
            if not isinstance(value, int):
                eng.to_reg(value)
            eng.wait_ge(s["const"], 1)
            eng.wait_ge(s[name], value)

        block = ctx.enter_context(nc.Block())

        @block.sync
        def _(sp):
            xv = x.rearrange("b (k p) c -> p b k c", p=P)
            xd = xres[:, :].rearrange("p (b k c) -> p b k c", b=B, c=C)
            sp.dma_start(xd[:, 0, 0:Q, :], xv[:, 0, 0:Q, :]).then_inc(s["x_first_in"], 16)
            for r, m in ((MAA_K, maa_k), (MAA_V, maa_v), (MAA_R, maa_r), (MAA_G, maa_g)):
                sp.dma_start(prow_maa[r:r + 1, :], m.rearrange("a b c -> (a b) c")).then_inc(s["params_in"], 16)
            for i, w in enumerate((wr, wk, wv, wg)):
                sp.dma_start(wraw[i], w).then_inc(s["params_in"], 16)
            sp.dma_start(dcol[:, 0:1], decay).then_inc(s["params_in"], 16)
            sp.dma_start(dcol[:, 1:2], faaaa).then_inc(s["params_in"], 16)
            sp.dma_start(xd[:, 0, Q:2 * Q, :], xv[:, 0, Q:2 * Q, :]).then_inc(s["x_other_in"], 16)
            sp.dma_start(woraw, wo).then_inc(s["other_params_in"], 16)
            for r, m in ((LN_W, ln_w), (LN_B, ln_b)):
                sp.dma_start(prow_rest[r - NB_MAA:r - NB_MAA + 1, :], m.rearrange("(a c) -> a c", a=1))\
                  .then_inc(s["other_params_in"], 16)
            sp.dma_start(prow_rest[BFC - NB_MAA:BFC - NB_MAA + E * J, :], bfc.rearrange("e (j p) -> (e j) p", p=P))\
              .then_inc(s["other_params_in"], 16)
            sp.dma_start(prow_rest[BFC - NB_MAA + E * J:NB - NB_MAA, :], bfc_s.rearrange("(j p) -> j p", p=P))\
              .then_inc(s["other_params_in"], 16)
            sp.dma_start(wrt[:, :], w_router).then_inc(s["other_params_in"], 16)
            sp.wait_ge(s["bias_zero"], 1)
            for g in range(3):
                sp.dma_start(bprow[g * PG:g * PG + E, :], bproj).then_inc(s["other_params_in"], 16)
                sp.dma_start(bprow[g * PG + E:g * PG + EXP, :], bproj_s.rearrange("(a c) -> a c", a=1))\
                  .then_inc(s["other_params_in"], 16)
            for b in range(1, B):
                sp.dma_start(xd[:, b, :, :], xv[:, b, :, :]).then_inc(s["x_second_in" if b == 1 else "x_rest_in"], 16)
            for e in range(EXP):
                sp.dma_start(w_stage(fc(e)), wfc[e] if e < E else wfc_s).then_inc(s["wexp_in"], 16)
                src = wproj[e] if e < E else wproj_s
                sp.dma_start(w_stage(proj(e)).rearrange("p (j c) -> p j c", c=C),
                             src.rearrange("(j p) c -> p j c", p=P)).then_inc(s["wexp_in"], 16)

            with sp.Fori(0, PAIRS) as i:
                for half in range(2):
                    sp.wait_ge(s["f_ob"], 2 * i + half + 1)
                    sp.dma_start(out[bass.ds(i, 1), half * TOK:(half + 1) * TOK, :]
                                 .rearrange("b (k p) c -> p (b k) c", p=P),
                                 ob.rearrange("p (k c) -> p k c", c=C)).then_inc(s["out_done"], 16)
            sp.wait_ge(s["out_done"], 16 * TILES)

        N_PARAMS = 16 * (4 + 4 + 2)
        N_OTHER_PARAMS = 16 * (1 + 2 + 2 + 1 + 3 * 2)

        @block.gpsimd
        def _(pool):
            pool.memset(ident[:, :], 0.0).then_inc(s["pool_set"], 1)
            pool.memset(sel[:, :], 1.0).then_inc(s["pool_set"], 1)
            pool.memset(selT[:, :], 1.0).then_inc(s["pool_set"], 1)
            pool.memset(neghalf[:, :], -0.5).then_inc(s["const"], 1)
            pool.iota(iota8[:, :], pattern=[[1, E]], base=0, channel_multiplier=0,
                      allow_small_or_imprecise_dtypes=True).then_inc(s["const"], 1)
            for i in range(2):
                pool.memset(gates[i][:, :, E:EXP], PROJ_DESCALE).then_inc(s["const"], 1)
            pool.memset(bprow[:, :], 0.0).then_inc(s["bias_zero"], 1)
            pool.wait_ge(s["pool_set"], 3)
            pool.affine_select(out=ident[:, :], in_=ident[:, :], compare_op=ALU.not_equal, fill=1.0,
                               base=0, pattern=[[-1, P]], channel_multiplier=1).then_inc(s["const"], 1)
            pool.affine_select(out=sel[:, :], in_=sel[:, :], compare_op=ALU.is_ge, fill=0.0,
                               base=0, pattern=[[-N, 32]], channel_multiplier=1).then_inc(s["pool_set"], 1)
            pool.affine_select(out=selT[:, :], in_=selT[:, :], compare_op=ALU.is_ge, fill=0.0,
                               base=0, pattern=[[1, P]], channel_multiplier=-N).then_inc(s["pool_set"], 1)
            pool.wait_ge(s["pool_set"], 5)
            pool.affine_select(out=sel[:, :], in_=sel[:, :], compare_op=ALU.is_ge, fill=0.0,
                               base=N - 1, pattern=[[N, 32]], channel_multiplier=-1).then_inc(s["const"], 1)
            pool.affine_select(out=selT[:, :], in_=selT[:, :], compare_op=ALU.is_ge, fill=0.0,
                               base=N - 1, pattern=[[-1, P]], channel_multiplier=N).then_inc(s["const"], 1)

            def rsqrt(var, ve, rs, eps, s_in, n_in, s_ve, s_rs, t):
                wait_apart(pool, s_in, n_in)
                pool.tensor_scalar(ve, var, 1.0, eps, ALU.mult, ALU.add).then_inc(s[s_ve], 1)
                pool.wait_ge(s[s_ve], t + 1)
                pool.tensor_tensor(rs, ve, neghalf[:, :], ALU.pow).then_inc(s[s_rs], 1)

            def variance(mv):
                return mv.rearrange("p (q two) -> p q two", two=2)[:, :, 1]

            def a_rstd(t, par):
                wait_past(pool, "a_xn", Q * t)
                rsqrt(variance(amv[par]), ave, ars, EPS_LN, "a_mv", Q * t + Q, "a_ve", "a_rstd", t)
                pool.tensor_scalar(anm, amv[par].rearrange("p (q two) -> p q two", two=2)[:, :, 0], -1.0, 0.0,
                                   ALU.mult, ALU.add).then_inc(s["a_nm"], 1)
                pool.wait_ge(s["a_rstd"], t + 1)
                pool.wait_ge(s["a_nm"], t + 1)
                pool.tensor_tensor(anmr, anm, ars, ALU.mult).then_inc(s["a_nmr"], 1)

            def a_shift(t, par, pair):
                pool.wait_ge(s["a_xT"], t + 1)
                if par:
                    pool.wait_ge(s["a_edge"], pair + 1)
                pool.tensor_tensor(xx, xT[par][:, 0:TOK], xT[par][:, 1:TOK + 1], ALU.subtract).then_inc(s["a_xx"], 1)

            def a_rs(t, par, m):
                n = N * t + m
                pool.wait_ge(s["a_sel"], n + 1)
                if m == 0:
                    pool.wait_ge(s["a_r"], t + 1)
                pool.wait_ge(s["a_scan"], n + 1)
                pool.tensor_tensor(rS[m % RS], S[m][:, 0:TOK], rch[par], ALU.mult).then_inc(s["a_rs"], 1)

            def a_ruk(t, par):
                wait_past(pool, "a_rk_ps", t)
                pool.wait_ge(s["a_r"], t + 1)
                pool.wait_ge(s["a_uk"], t + 1)
                pool.tensor_tensor(ruk, uk, rch[par], ALU.mult).then_inc(s["a_ruk"], 1)

            def a_tile(pair, par):
                t = 2 * pair + par
                last, ending = (is_int(t) and v for v in (t == TILES - 1, t >= TILES - 2))
                for m in range(N):
                    if m == 7 and not last:
                        a_ruk(t + 1, 1 - par)
                    if m == 0 and not last:
                        a_shift(t + 1, 1 - par, pair)
                    if last and m in (2, 4, 5, 6):
                        g_piece(0, 2 if m == 2 else m - 1, 0)
                    a_rs(t, par, m)
                    if m == 3 and not ending:
                        a_rstd(t + 2, par)

            def g_piece(u, e, up):
                if e == 2:
                    wait_apart(pool, "g_v", u + 1)
                    pool.tensor_scalar(gve, v64, 1.0 / N, EPS_GN, ALU.mult, ALU.add).then_inc(s["g_ve"], 1)
                    wait_apart(pool, "g_ve", u + 1)
                    pool.tensor_scalar(ghv, gve, -0.5, 0.0, ALU.mult, ALU.add).then_inc(s["g_hv"], 1)
                if 3 <= e < 3 + NEWTON:
                    n = 4 * NEWTON * u + 4 * (e - 3)
                    if e == 3:
                        pool.wait_ge(s["g_guess"], u + 1)
                        pool.wait_ge(s["g_hv"], u + 1)
                    else:
                        pool.wait_ge(s["g_newton"], n)
                    pool.tensor_tensor(gsq, grs, grs, ALU.mult).then_inc(s["g_newton"], 1)
                    pool.wait_ge(s["g_newton"], n + 1)
                    pool.tensor_tensor(gtm, gsq, ghv, ALU.mult).then_inc(s["g_newton"], 1)
                    wait_apart(pool, "g_newton", n + 2)
                    pool.tensor_scalar(gtf, gtm, 1.0, 1.5, ALU.mult, ALU.add).then_inc(s["g_newton"], 1)
                    pool.wait_ge(s["g_newton"], n + 3)
                    pool.tensor_tensor(grs, grs, gtf, ALU.mult).then_inc(s["g_newton"], 1)
                if e == 3 + NEWTON and not (is_int(u) and u == 0):
                    wait_past(pool, "b_ynT", u - 1)
                    pool.wait_ge(s["g_newton"], 4 * NEWTON * (u + 1))
                    pool.tensor_tensor(yn[up].rearrange("p (h m) -> p h m", m=N),
                                       yc.rearrange("p (h m) -> p h m", m=N),
                                       grs.unsqueeze(2).to_broadcast([P, Q * H, N]), ALU.mult).then_inc(s["g_yn"], 1)

            def b_gate(u):
                pool.wait_ge(s["b_zT"], u + 1)
                pool.tensor_tensor(zz, zT, tile_of(gres, u), ALU.mult).then_inc(s["b_zz"], 1)

            def b_ors(u):
                rsqrt(variance(omv), ove, ors, EPS_LN, "b_omv", Q * u + Q, "b_ove", "b_ors", u)

            def b_x1(u):
                pool.wait_ge(s["b_dd"], Q * u + Q)
                pool.tensor_tensor(tile_of(xres, u), tile_of(xres, u), dd, ALU.add).then_inc(s["b_x1"], 1)

            def b_xrs(u):
                rsqrt(variance(xmv), xve, xrs, EPS_LN, "b_xmv", Q * u + Q, "b_xve", "b_xrs", u)

            def f_rs(t):
                rsqrt(variance(fmv), fve, frs, EPS_LN, "f_mv", Q * t + Q, "f_ve", "f_rs", t)

            def f_out(t):
                pool.wait_ge(s["f_dd"], Q * t + Q)
                wait_past(pool, "out_done", 16 * t)
                pool.tensor_tensor(ob, tile_of(xres, t), dd2, ALU.add).then_inc(s["f_ob"], 1)

            def b_hi(t, g, j, par):
                n = J * g + j
                if j == 0:
                    pool.wait_ge(s["b_proj"], g + 1)
                wait_apart(pool, "b_gelu", n + 1)
                pool.tensor_scalar(hh[par][j], h32[j], H_SCALE, 0.0, ALU.mult, ALU.add).then_inc(s["b_hi"], 1)

            def b_piece(u, e):
                first = is_int(u) and u == 0
                if e == 2 and not first:
                    b_gate(u)
                if e == 3:
                    b_ors(u)
                if e == 4 and not first:
                    b_x1(u)
                if e == 5:
                    b_xrs(u)

            def f_piece(t, e):
                if e == 1:
                    f_rs(t)
                if e == 2:
                    f_out(t)

            def b_tile(t, tp):
                for e in range(EXP):
                    for j in range(J):
                        b_hi(t, EXP * t + e, j, (EXP * tp + e) % 2)
                    if is_int(t) and t == 0 and e == 0:
                        for n in range(3, 3 + NEWTON + 1):
                            g_piece(1, n, 1)
                    if not is_int(t) or t + 1 < TILES:
                        b_piece(t + 1, e)
                    if not is_int(t) or t > 0:
                        f_piece(t - 1, e)
                    if not is_int(t) or t + 2 < TILES:
                        g_piece(t + 2, e, tp)

            pool.wait_ge(s["const"], 7)
            a_rstd(0, 0)
            pool.wait_ge(s["xt0_zero"], 1)
            a_shift(0, 0, 0)
            a_rstd(1, 1)
            a_ruk(0, 0)
            a_tile(0, 0)
            a_tile(0, 1)
            with pool.Fori(1, PAIRS - 1) as i:
                a_tile(i, 0)
                a_tile(i, 1)
            a_tile(PAIRS - 1, 0)
            a_tile(PAIRS - 1, 1)

            for e in range(EXP):
                b_piece(0, e)
            g_piece(1, 2, 1)
            b_tile(0, 0)
            b_tile(1, 1)
            with pool.Fori(1, PAIRS - 1) as i:
                b_tile(2 * i, 0)
                b_tile(2 * i + 1, 1)
            b_tile(TILES - 2, 0)
            b_tile(TILES - 1, 1)
            for e in range(EXP):
                f_piece(TILES - 1, e)

        @block.scalar
        def _(act):
            def copy(o, i):
                return act.activation(o, i, ACT.Copy)

            def a_xT(t, par):
                act.wait_ge(s["a_xT_ps"], t + 1)
                copy(xT[par][:, 1:TOK + 1], bkA[:, :]).then_inc(s["a_xT"], 1)
                if par:
                    wait_past(act, "a_xT", t)
                    copy(xT[1][:, 0:1], xT[0][:, TOK:TOK + 1]).then_inc(s["a_edge"], 1)

            def a_xn(t):
                wait_past(act, "a_xT_ps", t)
                act.wait_ge(s["a_nmr"], t + 1)
                for q in range(Q):
                    act.activation(xn[:, q * P:(q + 1) * P], chunk_of(xres, t, q), ACT.Identity,
                                   bias=anmr[:, q:q + 1], scale=ars[:, q:q + 1]).then_inc(s["a_xn"], 1)

            def split(i):
                if i == 0:
                    act.wait_ge(s["wexp_in"], 16 * 2 * EXP)
                else:
                    act.wait_ge(s["split_lo"], i)
                act.activation(w_hi(i), w_stage(i), ACT.Copy, scale=W_SCALE).then_inc(s["split_hi"], 1)

            def a_k(t, par):
                act.wait_ge(s["a_k_ps"], t + 1)
                copy(kch[par], bkC[:, :]).then_inc(s["a_k"], 1)
                wait_past(act, "a_ruk", t)
                act.activation(uk, bkC[:, :], ACT.Copy, scale=ucol[:, 0:1]).then_inc(s["a_uk"], 1)

            def a_r(t, par):
                act.wait_ge(s["a_r_ps"], t + 1)
                copy(rch[par], bkB[:, :]).then_inc(s["a_r"], 1)

            def a_g(t):
                act.wait_ge(s["a_g_ps"], t + 1)
                act.activation(tile_of(gres, t), bkD[:, :], ACT.Gelu).then_inc(s["a_g"], 1)

            def a_rk(t):
                act.wait_ge(s["a_rk_ps"], t + 1)
                wait_past(act, "a_yu", t)
                copy(rk, bkB[:, 0:Q * H]).then_inc(s["a_rk"], 1)

            def a_yev(t, b):
                act.wait_ge(s["a_sel"], N * t + N // 2 * (b + 1) + RS)
                copy(ych[b], bkY[b][:, :]).then_inc(s["a_yev"], 1)

            def a_tile(t, par, first, last, ending):
                if not last:
                    a_xT(t + 1, 1 - par)
                else:
                    g_piece(0, 1)
                a_rk(t)
                if not first:
                    a_yev(t - 1, 1)
                if is_int(t) and t == TILES - 2:
                    split(0)
                if last:
                    split(1)
                    split(2)
                a_yev(t, 0)
                if last:
                    split(3)
                if not last:
                    a_k(t + 1, 1 - par)
                if not ending:
                    a_xn(t + 2)
                if not last:
                    a_r(t + 1, 1 - par)
                    a_g(t + 1)

            def g_piece(u, e):
                if e == 1:
                    act.wait_ge(s["g_yc"], u + 1)
                    act.activation(sq, yc, ACT.Square).then_inc(s["g_sq"], 1)

            def b_piece(u, e, up):
                if e == 1:
                    act.wait_ge(s["b_ynT"], u + 1)
                    act.activation(zT, bkX[:, :], ACT.Identity, bias=pcol[:, LN_B:LN_B + 1],
                                   scale=pcol[:, LN_W:LN_W + 1]).then_inc(s["b_zT"], 1)
                if e == 6:
                    act.wait_ge(s["b_xn2T"], u + 1)
                    act.activation(xh[up], bkX[:, :], ACT.Copy, scale=X_SCALE).then_inc(s["b_xh"], 1)
                if e == 8:
                    act.wait_ge(s["b_lgd"], u + 1)
                    act.activation(ex, lg, ACT.Exp, scale=FC_DESCALE).then_inc(s["b_ex"], 1)

            def b_g3T(u):
                act.wait_ge(s["b_gT"], u + 1)
                copy(g3T, bkX[0:3 * PG, :]).then_inc(s["b_g3T"], 1)

            def b_bias(u, up):
                wait_past(act, "f_dd", Q * (u - 1))
                act.wait_ge(s["b_bias"], u + 1)
                act.activation(acc[up], bkZ[:, :], ACT.Copy, scale=BIAS_DESCALE).then_inc(s["b_acc"], 1)

            def b_gelu(g, e, j):
                n = J * g + j
                act.wait_ge(s["b_fc"], n + 1)
                act.wait_ge(s["b_lo"], n + 1)
                b = BFC + e * J + j
                act.activation(h32[j], bkF[j][:, :], ACT.Gelu_apprx_tanh, bias=pcol[:, b:b + 1],
                               scale=FC_DESCALE).then_inc(s["b_gelu"], 1)

            def b_tile(t, tp):
                for e in range(EXP):
                    for j in range(J):
                        b_gelu(EXP * t + e, e, j)
                    if e == 0:
                        b_g3T(t)
                        b_bias(t, tp)
                    if is_int(t) and t == 0:
                        for i in chunks_at(e):
                            split(i)
                    if not is_int(t) or t + 1 < TILES:
                        b_piece(t + 1, e, 1 - tp)
                    if not is_int(t) or t + 2 < TILES:
                        g_piece(t + 2, e)

            a_xn(0)
            a_xT(0, 0)
            act.wait_ge(s["decay_ps"], 1)
            act.activation(dexp[:, 0:1], bkV[0][:, 0:1], ACT.Exp).then_inc(s["decay_e"], 1)
            copy(ucol[:, :], bkV[0][:, 1:2]).then_inc(s["decay_r"], 1)
            act.wait_ge(s["decay_e"], 1)
            act.activation(wcol[:, :], dexp[:, 0:1], ACT.Exp, scale=-1.0).then_inc(s["decay_r"], 1)
            act.wait_ge(s["setup_t"], 1)
            copy(pcol[:, 0:NB_MAA], bkV[1][:, 0:NB_MAA]).then_inc(s["setup_ev"], 1)
            for n in range(4):
                act.wait_ge(s["setup_t"], n + 2)
                copy(wt[:, n, :], bank[n][:, 0:C]).then_inc(s["setup_ev"], 1)
            a_xn(1)
            a_k(0, 0)
            a_r(0, 0)
            a_g(0)
            act.wait_ge(s["other_params_in"], N_OTHER_PARAMS)
            act.activation(bps[:, :], bprow[:, :], ACT.Copy, scale=W_SCALE).then_inc(s["late_ev"], 1)
            act.activation(wrt_hi[:, :], wrt[:, :], ACT.Copy, scale=W_SCALE).then_inc(s["late_ev"], 1)
            act.wait_ge(s["late_t"], 1)
            copy(wt[:, O_, :], bank[0][:, 0:C]).then_inc(s["late_ev"], 1)
            act.wait_ge(s["late_t"], 2)
            copy(pcol[:, NB_MAA:NB], bank[1][:, 0:NB - NB_MAA]).then_inc(s["late_ev"], 1)
            a_tile(0, 0, True, False, False)
            a_tile(1, 1, False, False, False)
            with act.Fori(1, PAIRS - 1) as i:
                a_tile(2 * i, 0, False, False, False)
                a_tile(2 * i + 1, 1, False, False, False)
            a_tile(TILES - 2, 0, False, False, True)
            a_tile(TILES - 1, 1, False, True, True)
            split(4)
            b_piece(0, 1, 0)
            split(5)
            split(6)
            a_yev(TILES - 1, 1)
            for i in range(7, 10):
                split(i)
            b_piece(0, 6, 0)
            g_piece(1, 1)
            split(10)
            b_piece(0, 8, 0)
            split(11)
            b_tile(0, 0)
            b_tile(1, 1)
            with act.Fori(1, PAIRS - 1) as i:
                b_tile(2 * i, 0)
                b_tile(2 * i + 1, 1)
            b_tile(TILES - 2, 0)
            b_tile(TILES - 1, 1)

        @block.vector
        def _(dve):
            def sub_scale(o, i, mean, rstd):
                return dve.tensor_scalar(o, i, mean, rstd, ALU.subtract, ALU.mult)

            dve.memset(xT[0][:, 0:1], 0.0).then_inc(s["xt0_zero"], 1)
            dve.memset(kv[0][:, 0:1], 0.0).then_inc(s["a_sel"], RS)
            dve.memset(kv[0][:, 1:2], 0.0).then_inc(s["b_lo"], J)
            dve.memset(kv[0][:, 2:3], 0.0).then_inc(s["b_proj"], 2)
            dve.memset(kv[0][:, 3:4], 0.0).then_inc(s["b_comb"], 2 * Q)

            def a_stats(t, par):
                wait_past(dve, "a_mv", Q * t)
                for q in range(Q):
                    dve.bn_stats(ast[:, 6 * q:6 * q + 6], chunk_of(xres, t, q)).then_inc(s["a_stats"], 1)

            def a_moments(t, par):
                wait_past(dve, "a_nmr", t - 1)
                wait_apart(dve, "a_stats", Q * t + Q)
                for q in range(Q):
                    dve.bn_aggr(amv[par][:, 2 * q:2 * q + 2], ast[:, 6 * q:6 * q + 6]).then_inc(s["a_mv"], 1)

            def a_mix(t, par, n, col):
                if n == 0:
                    dve.wait_ge(s["a_xx"], t + 1)
                if n:
                    wait_past(dve, ("a_k_ps", "a_r_ps", "a_g_ps")[n - 1], t)
                dve.scalar_tensor_tensor(out=(xmix_v[par], xmix_k, xmix_r, xmix_g)[n], in0=xx,
                                         scalar=pcol[:, col:col + 1], in1=xT[par][:, 1:TOK + 1], op0=ALU.mult, op1=ALU.add).then_inc(s["a_mix"], 1)

            MIX = (MAA_V, MAA_K, MAA_R, MAA_G)
            MIX_AT = (2, 3, 5, 6)

            def a_kv(t, par, m):
                n = N * t + m
                dve.wait_ge(s["a_vrep"], n + 1)
                if m == 0:
                    dve.wait_ge(s["a_k"], t + 1)
                dve.tensor_tensor(kv[m % 2], bkV[m % 2][:, :], kch[par], ALU.mult).then_inc(s["a_kv"], 1)
                if par:
                    dve.wait_ge(s["a_rs"], n - N + 1)
                    dve.tensor_copy(S[m][:, 0:1], S[m][:, TOK:TOK + 1]).then_inc(s["a_carry"], 1)
                else:
                    wait_past(dve, "a_rs", n - N + 1)
                    dve.memset(S[m][:, 0:1], 0.0).then_inc(s["a_carry"], 1)

            def a_scan(t, m):
                n = N * t + m
                dve.wait_ge(s["a_kv"], n + 1)
                dve.wait_ge(s["a_carry"], n + 1)
                dve.tensor_tensor_scan(S[m][:, 1:TOK + 1], wcol[:, 0:1].to_broadcast([P, TOK]), kv[m % 2],
                                       S[m][:, 0:1], ALU.mult, ALU.add).then_inc(s["a_scan"], 1)

            def split(i):
                dve.wait_ge(s["split_hi"], i + 1)
                dve.scalar_tensor_tensor(out=w_lo(i), in0=w_stage(i), scalar=W_SCALE, in1=w_hi(i),
                                         op0=ALU.mult, op1=ALU.subtract).then_inc(s["split_lo"], 1)

            def a_yu(t):
                dve.wait_ge(s["a_vt"], t + 1)
                dve.wait_ge(s["a_rk"], t + 1)
                dve.tensor_tensor(tile_of(yres, t).rearrange("p (h m) -> p h m", m=N),
                                  bkA[:, :].rearrange("p (h m) -> p h m", m=N),
                                  rk.unsqueeze(2).to_broadcast([P, Q * H, N]), ALU.mult).then_inc(s["a_yu"], 1)

            def a_y(t):
                dve.wait_ge(s["a_yu"], t + 1)
                for b in range(2):
                    dve.wait_ge(s["a_yT"], 2 * t + b + 1)
                    y = tile_of(yres, t).rearrange("p (q h b g) -> p q h b g", h=H, b=2, g=4)[:, :, :, b, :]
                    ps = (bkC, bkD)[b][:, :].rearrange("p (q g h) -> p q h g", g=4, h=32)[:, :, 0:H, :]
                    dve.tensor_tensor(y, ps, y, ALU.add).then_inc(s["a_y"], 1)

            def a_tile(t, par):
                first, last, ending = (is_int(t) and v for v in (t == 0, t == TILES - 1, t >= TILES - 2))
                for m in range(N):
                    a_kv(t, par, m)
                    if m == 0 and not ending:
                        if is_int(t) and t == 0:
                            dve.wait_ge(s["x_second_in"], 16)
                        a_stats(t + 2, par)
                    if m == 1 and not ending:
                        a_moments(t + 2, par)
                    if m in MIX_AT and not last:
                        n = MIX_AT.index(m)
                        a_mix(t + 1, 1 - par, n, MIX[n])
                    if m == 4 and not first:
                        a_y(t - 1)
                    if m == 4 and ending and not last:
                        split(0)
                    if last:
                        if m in (0, 2, 3):
                            g_piece(0, (m + 1) // 2)
                        if m in (3, 5, 6):
                            split(m - 2 if m == 3 else m - 3)
                        if m == 7:
                            g_yn0()
                    if m == (5 if last else 7):
                        a_yu(t)
                    a_scan(t, m)

            def stats(src, st, mv, s_st, s_mv, t):
                for q in range(Q):
                    dve.bn_stats(st[:, 6 * q:6 * q + 6], src(q)).then_inc(s[s_st], 1)
                wait_apart(dve, s_st, Q * t + Q)
                for q in range(Q):
                    dve.bn_aggr(mv[:, 2 * q:2 * q + 2], st[:, 6 * q:6 * q + 6]).then_inc(s[s_mv], 1)

            def normalise(dst, src, mv, rs, s_out):
                for q in range(Q):
                    sub_scale(dst[:, q * P:(q + 1) * P], src(q), mv[:, 2 * q:2 * q + 1],
                              rs[:, q:q + 1]).then_inc(s[s_out], 1)

            def per_expert(a):
                return a.rearrange("p (q e) -> p q e", e=E)

            def gates_part(g):
                return g3.rearrange("p (q g e) -> p q g e", g=3, e=PG)[:, :, g, 0:EXP]

            def over_experts(a):
                return a.unsqueeze(2).to_broadcast([P, Q, E])

            def g_piece(u, e):
                y3 = tile_of(yres, u).rearrange("p (h m) -> p h m", m=N)
                if e == 0:
                    dve.tensor_reduce(s64, y3, AX.X, ALU.add).then_inc(s["g_s"], 1)
                    wait_past(dve, "g_yn", u)
                    dve.wait_ge(s["g_s"], u + 1)
                    dve.scalar_tensor_tensor(out=yc.rearrange("p (h m) -> p h m", m=N),
                                             in0=s64.unsqueeze(2).to_broadcast([P, Q * H, N]), scalar=-1.0 / N,
                                             in1=y3, op0=ALU.mult, op1=ALU.add).then_inc(s["g_yc"], 1)
                if e == 1:
                    dve.wait_ge(s["g_sq"], u + 1)
                    dve.tensor_reduce(v64, sq.rearrange("p (h m) -> p h m", m=N), AX.X, ALU.add).then_inc(s["g_v"], 1)
                if e == 2:
                    dve.wait_ge(s["g_ve"], u + 1)
                    dve.tensor_scalar(gshift, gve.bitcast(U32), 1, None, ALU.logical_shift_right)\
                       .then_inc(s["g_shift"], 1)
                    dve.wait_ge(s["g_shift"], u + 1)
                    dve.tensor_scalar(grs.bitcast(U32), gshift, -1.0, float(GUESS), ALU.mult, ALU.add)\
                       .then_inc(s["g_guess"], 1)

            def g_yn0():
                dve.wait_ge(s["g_newton"], 4 * NEWTON)
                dve.tensor_tensor(yn[0].rearrange("p (h m) -> p h m", m=N), yc.rearrange("p (h m) -> p h m", m=N),
                                  grs.unsqueeze(2).to_broadcast([P, Q * H, N]), ALU.mult).then_inc(s["g_yn"], 1)

            def b_zz0():
                dve.wait_ge(s["b_zT"], 1)
                dve.tensor_tensor(zz, zT, tile_of(gres, 0), ALU.mult).then_inc(s["b_zz"], 1)

            def b_x10():
                dve.wait_ge(s["b_dd"], Q)
                dve.tensor_tensor(tile_of(xres, 0), tile_of(xres, 0), dd, ALU.add).then_inc(s["b_x1"], 1)

            def b_piece(u, e, up):
                if e == 2:
                    dve.wait_ge(s["b_o"], u + 1)
                    stats(lambda q: bkZ[:, q * P:(q + 1) * P], ost, omv, "b_ost", "b_omv", u)
                if e == 3:
                    dve.wait_ge(s["b_ors"], u + 1)
                    normalise(dd, lambda q: bkZ[:, q * P:(q + 1) * P], omv, ors, "b_dd")
                if e == 4:
                    dve.wait_ge(s["b_x1"], u + 1)
                    stats(lambda q: chunk_of(xres, u, q), xst, xmv, "b_xst", "b_xmv", u)
                if e == 5:
                    dve.wait_ge(s["b_xrs"], u + 1)
                    normalise(xn2, lambda q: chunk_of(xres, u, q), xmv, xrs, "b_xn2")
                if e == 6:
                    dve.wait_ge(s["b_xh"], u + 1)
                    dve.scalar_tensor_tensor(out=xl[up], in0=bkX[:, :], scalar=X_SCALE, in1=xh[up],
                                             op0=ALU.mult, op1=ALU.subtract).then_inc(s["b_xl"], 1)
                if e == 7:
                    dve.wait_ge(s["b_lg"], u + 1)
                    z3 = bkZ[:, 0:Q * E].rearrange("p (q e) -> p q e", e=E)
                    dve.tensor_reduce(mx, z3, AX.X, ALU.max).then_inc(s["b_mx"], 1)
                    dve.wait_ge(s["b_mx"], u + 1)
                    dve.tensor_tensor(per_expert(lg), z3, over_experts(mx), ALU.subtract).then_inc(s["b_lgd"], 1)
                if e == 8:
                    dve.wait_ge(s["b_ex"], u + 1)
                    dve.tensor_reduce(se, per_expert(ex), AX.X, ALU.add).then_inc(s["b_se"], 1)
                    dve.wait_ge(s["b_se"], u + 1)
                    dve.reciprocal(rse, se).then_inc(s["b_rse"], 1)
                    dve.wait_ge(s["b_rse"], u + 1)
                    dve.tensor_tensor(per_expert(pr), per_expert(ex), over_experts(rse), ALU.mult)\
                       .then_inc(s["b_pr"], 1)
                    wait_apart(dve, "b_pr", u + 1)
                    for q in range(Q):
                        dve.max(top[:, 8 * q:8 * q + 8], pr[:, E * q:E * q + E]).then_inc(s["b_top"], 1)
                    wait_apart(dve, "b_top", Q * u + Q)
                    for q in range(Q):
                        dve.max_index(tix[:, 8 * q:8 * q + 8], top[:, 8 * q:8 * q + 8], pr[:, E * q:E * q + E])\
                           .then_inc(s["b_tix"], 1)
                    top3 = top.rearrange("p (q k) -> p q k", k=8)
                    dve.tensor_tensor(s2.unsqueeze(2), top3[:, :, 0:1], top3[:, :, 1:2], ALU.add)\
                       .then_inc(s["b_s2"], 1)
                    dve.wait_ge(s["b_s2"], u + 1)
                    dve.reciprocal(r2, s2).then_inc(s["b_r2"], 1)
                    dve.wait_ge(s["b_tix"], Q * u + Q)
                    dve.tensor_copy(tif, tix).then_inc(s["b_eq"], 1)
                    dve.wait_ge(s["b_r2"], u + 1)
                    g23 = g2.rearrange("p (q k) -> p q k", k=2)
                    dve.scalar_tensor_tensor(out=g23, in0=top3[:, :, 0:2], scalar=PROJ_DESCALE,
                                             in1=r2.unsqueeze(2).to_broadcast([P, Q, 2]), op0=ALU.mult,
                                             op1=ALU.mult).then_inc(s["b_g2"], 1)
                    dve.wait_ge(s["b_eq"], 5 * u + 1)
                    tif3 = tif.rearrange("p (q k) -> p q k", k=8)
                    io = iota8[:, :].unsqueeze(1).to_broadcast([P, Q, E])
                    for k in range(2):
                        dve.tensor_tensor(per_expert(eq[k]), io, tif3[:, :, k:k + 1].to_broadcast([P, Q, E]),
                                          ALU.is_equal).then_inc(s["b_eq"], 1)
                    dve.wait_ge(s["b_g2"], u + 1)
                    for k in range(2):
                        dve.wait_ge(s["b_eq"], 5 * u + 2 + k)
                        dve.tensor_tensor(per_expert(eq[k]), per_expert(eq[k]),
                                          g23[:, :, k:k + 1].to_broadcast([P, Q, E]), ALU.mult)\
                           .then_inc(s["b_eq"], 1)
                    dve.wait_ge(s["b_eq"], 5 * u + 5)
                    dve.tensor_tensor(gates[up][:, :, 0:E], per_expert(eq[0]), per_expert(eq[1]), ALU.add)\
                       .then_inc(s["b_gate"], 1)
                    dve.wait_ge(s["b_gate"], u + 1)
                    wait_past(dve, "b_gT", u)
                    gq = G_SCALE / PROJ_DESCALE
                    g16q = g16.rearrange("p (q e) -> p q e", e=EXP)
                    dve.tensor_scalar(g16q, gates[up][:, :, :], gq, 0.0, ALU.mult, ALU.add).then_inc(s["b_g16"], 1)
                    dve.wait_ge(s["b_g16"], u + 1)
                    dve.tensor_copy(gates_part(0), g16q).then_inc(s["b_g3"], 1)
                    dve.tensor_copy(gates_part(2), g16q).then_inc(s["b_g3"], 1)
                    dve.scalar_tensor_tensor(out=gates_part(1), in0=gates[up][:, :, :], scalar=gq, in1=g16q,
                                             op0=ALU.mult, op1=ALU.subtract).then_inc(s["b_g3"], 1)

            def b_lo(g, j, par):
                n = J * g + j
                dve.wait_ge(s["b_hi"], n + 1)
                dve.scalar_tensor_tensor(out=hl[par][j], in0=h32[j], scalar=H_SCALE, in1=hh[par][j],
                                         op0=ALU.mult, op1=ALU.subtract).then_inc(s["b_lo"], 1)

            def b_comb(t, g, e, tp, par):
                dve.wait_ge(s["b_proj"], g + 1 + 2)
                if e == 0:
                    dve.wait_ge(s["b_acc"], t + 1)
                for q in range(Q):
                    a = acc[tp][:, q * P:(q + 1) * P]
                    dve.wait_ge(s["b_comb"], Q * g + q + 1 - Q + 2 * Q)
                    dve.scalar_tensor_tensor(out=a, in0=bkP[par][:, q * P:(q + 1) * P],
                                             scalar=gates[tp][:, q, e:e + 1], in1=a,
                                             op0=ALU.mult, op1=ALU.add).then_inc(s["b_comb"], 1)

            def f_stats(t, tp):
                dve.wait_ge(s["b_comb"], Q * EXP * (t + 1) + 2 * Q)
                stats(lambda q: acc[tp][:, q * P:(q + 1) * P], fst, fmv, "f_st", "f_mv", t)

            def f_norm(t, tp):
                dve.wait_ge(s["f_rs"], t + 1)
                wait_past(dve, "f_ob", t)
                normalise(dd2, lambda q: acc[tp][:, q * P:(q + 1) * P], fmv, frs, "f_dd")

            def b_tile(t, tp):
                for e in range(EXP):
                    g = EXP * t + e
                    par = (EXP * tp + e) % 2
                    for j in range(J):
                        b_lo(g, j, par)
                    if e:
                        b_comb(t, g - 1, e - 1, tp, 1 - par)
                    if is_int(t) and t == 0:
                        for i in chunks_at(e):
                            split(i)
                    if not is_int(t) or t > 0:
                        if e == 0:
                            b_comb(t - 1, g - 1, EXP - 1, 1 - tp, 1 - par)
                            f_stats(t - 1, 1 - tp)
                        if e == 1:
                            f_norm(t - 1, 1 - tp)
                    if not is_int(t) or t + 1 < TILES:
                        b_piece(t + 1, e, 1 - tp)
                    if not is_int(t) or t + 2 < TILES:
                        g_piece(t + 2, e)

            dve.wait_ge(s["x_first_in"], 16)
            a_stats(0, 0)
            a_moments(0, 0)
            dve.wait_ge(s["x_other_in"], 16)
            a_stats(1, 1)
            a_moments(1, 1)
            dve.wait_ge(s["setup_ev"], 1)
            for n in range(2):
                a_mix(0, 0, n, MIX[n])
            dve.wait_ge(s["setup_ev"], 5)
            for m in range(N):
                src = wt[:, V_, :].rearrange("p (h m) -> p h m", m=N)[:, :, m:m + 1].to_broadcast([P, H, N])
                dve.tensor_copy(wvrep[:, m, :].rearrange("p (h n) -> p h n", n=N), src).then_inc(s["wvrep_done"], 1)
            for n in range(2, 4):
                a_mix(0, 0, n, MIX[n])
            dve.wait_ge(s["decay_r"], 2)
            a_tile(0, 0)
            dve.wait_ge(s["late_ev"], 2)
            dve.scalar_tensor_tensor(out=wrt_lo[:, :], in0=wrt[:, :], scalar=W_SCALE, in1=wrt_hi[:, :],
                                     op0=ALU.mult, op1=ALU.subtract).then_inc(s["late_lo"], 1)
            low = slice(2 * PG, 3 * PG)
            dve.scalar_tensor_tensor(out=bps[low, :], in0=bprow[low, :], scalar=W_SCALE, in1=bps[low, :],
                                     op0=ALU.mult, op1=ALU.subtract).then_inc(s["late_lo"], 1)
            a_tile(1, 1)
            dve.wait_ge(s["x_rest_in"], 16 * (B - 2))
            with dve.Fori(1, PAIRS - 1) as i:
                a_tile(2 * i, 0)
                a_tile(2 * i + 1, 1)
            a_tile(TILES - 2, 0)
            a_tile(TILES - 1, 1)
            split(4)
            dve.memset(g3, 0.0).then_inc(s["g3_zero"], 1)
            b_zz0()
            split(5)
            split(6)
            b_piece(0, 2, 0)
            split(7)
            b_piece(0, 3, 0)
            b_x10()
            b_piece(0, 4, 0)
            a_y(TILES - 1)
            split(8)
            b_piece(0, 5, 0)
            split(9)
            g_piece(1, 0)
            b_piece(0, 6, 0)
            b_piece(0, 7, 0)
            split(10)
            g_piece(1, 1)
            g_piece(1, 2)
            b_piece(0, 8, 0)
            split(11)
            b_tile(0, 0)
            b_tile(1, 1)
            with dve.Fori(1, PAIRS - 1) as i:
                b_tile(2 * i, 0)
                b_tile(2 * i + 1, 1)
            b_tile(TILES - 2, 0)
            b_tile(TILES - 1, 1)
            b_comb(TILES - 1, EXP * TILES - 1, EXP - 1, 1, (EXP * TILES - 1) % 2)
            f_stats(TILES - 1, 1)
            f_norm(TILES - 1, 1)

        @block.tensor
        def _(pe):
            def mm(o, lhsT, rhs, start=True, stop=True, **k):
                return pe.matmul(o, lhsT, rhs, start=start, stop=stop, **k)

            pe.wait_ge(s["const"], 7)
            pe.wait_ge(s["a_xn"], Q)
            for q in range(Q):
                i = pe.transpose(bkA[:, q * P:(q + 1) * P], xn[:, q * P:(q + 1) * P], ident[:, :])
            i.then_inc(s["a_xT_ps"], 1)
            pe.wait_ge(s["params_in"], N_PARAMS)
            mm(bkV[0][:, 0:2], selT[:, :], dcol[:, :]).then_inc(s["decay_ps"], 1)
            pe.transpose(bkV[1][:, 0:NB_MAA], prow_maa, ident[0:NB_MAA, 0:NB_MAA]).then_inc(s["setup_t"], 1)
            for n in range(4):
                pe.transpose(bank[n][:, 0:C], wraw[n], ident[:, :]).then_inc(s["setup_t"], 1)

            def a_T(t):
                pe.wait_ge(s["a_xn"], Q * t + Q)
                wait_past(pe, "a_yu", t - 1)
                for q in range(Q):
                    i = pe.transpose(bkA[:, q * P:(q + 1) * P], xn[:, q * P:(q + 1) * P], ident[:, :])
                i.then_inc(s["a_xT_ps"], 1)

            def a_k(t):
                pe.wait_ge(s["a_mix"], 4 * t + 2)
                wait_past(pe, "a_y", 2 * t - 2)
                mm(bkC[:, :], wt[:, K_, :], xmix_k).then_inc(s["a_k_ps"], 1)

            def a_r(t):
                pe.wait_ge(s["a_mix"], 4 * t + 3)
                wait_past(pe, "a_rk", t)
                mm(bkB[:, :], wt[:, R_, :], xmix_r).then_inc(s["a_r_ps"], 1)

            def a_g(t):
                pe.wait_ge(s["a_mix"], 4 * t + 4)
                mm(bkD[:, :], wt[:, G_, :], xmix_g).then_inc(s["a_g_ps"], 1)

            def a_vrep(t, par, m, lead):
                if not lead:
                    pe.wait_ge(s["a_kv"], N * t + m - 1)
                mm(bkV[m % 2][:, :], wvrep[:, m, :], xmix_v[par]).then_inc(s["a_vrep"], 1)

            def a_sel(t, m):
                if m % 4 == 0:
                    wait_past(pe, "a_yev", 2 * t - 1 + m // 4)
                pe.wait_ge(s["a_rs"], N * t + m + 1)
                g = 32 * (m % 4)
                mm(bkY[m // 4][g:g + 32, :], sel[:, :], rS[m % RS]).then_inc(s["a_sel"], 1)

            def a_vtok(t, par, last):
                pe.wait_ge(s["a_xT"], t + 1 if last else t + 2)
                for q in range(Q):
                    i = mm(bkA[:, q * P:(q + 1) * P], xmix_v[par][:, q * P:(q + 1) * P], wt[:, V_, :])
                i.then_inc(s["a_vt"], 1)

            def a_rk(t):
                pe.wait_ge(s["a_ruk"], t + 1)
                for q in range(Q):
                    i = mm(bkB[:, q * H:(q + 1) * H], ruk[:, q * P:(q + 1) * P], sel[:, 0:H])
                i.then_inc(s["a_rk_ps"], 1)

            def a_yT(t):
                for b in range(2):
                    pe.wait_ge(s["a_yev"], 2 * t + b + 1)
                    if not is_int(t) or t + 1 < TILES:
                        pe.wait_ge(s["a_g" if b else "a_uk"], t + 2)
                    for q in range(Q):
                        i = pe.transpose((bkC, bkD)[b][:, q * P:(q + 1) * P], ych[b][:, q * P:(q + 1) * P],
                                         ident[:, :])
                    i.then_inc(s["a_yT"], 1)

            def a_tile(t, par, first, last):
                for m in range(N):
                    if m == 0 and not last:
                        a_T(t + 1)
                    if m + 2 < N:
                        a_vrep(t, par, m + 2, False)
                    elif not last:
                        a_vrep(t + 1, 1 - par, m + 2 - N, False)
                    if m == 2 and first:
                        pe.wait_ge(s["late_ev"], 4)
                    if m >= 2:
                        a_sel(t, m - 2)
                    elif not first:
                        a_sel(t - 1, m + N - 2)
                    if m == 1:
                        a_rk(t)
                    if m == 2 and not first:
                        a_yT(t - 1)
                    if m == 3:
                        a_vtok(t, par, last)
                    if m == 5 and not last:
                        a_k(t + 1)
                    if m == 6 and not last:
                        a_r(t + 1)
                    if m == 7 and not last:
                        a_g(t + 1)

            def b_piece(u, e, up):
                if e == 1:
                    wait_past(pe, "b_g3T", u)
                    pe.wait_ge(s["g_yn"], u + 1)
                    for q in range(Q):
                        i = pe.transpose(bkX[:, q * P:(q + 1) * P], yn[up][:, q * P:(q + 1) * P], ident[:, :])
                    i.then_inc(s["b_ynT"], 1)
                if e == 2:
                    wait_past(pe, "b_acc", u)
                    pe.wait_ge(s["b_zz"], u + 1)
                    for q in range(Q):
                        i = mm(bkZ[:, q * P:(q + 1) * P], zz[:, q * P:(q + 1) * P], wt[:, O_, :])
                    i.then_inc(s["b_o"], 1)
                if e == 6:
                    pe.wait_ge(s["b_xn2"], Q * u + Q)
                    for q in range(Q):
                        i = pe.transpose(bkX[:, q * P:(q + 1) * P], xn2[:, q * P:(q + 1) * P], ident[:, :])
                    i.then_inc(s["b_xn2T"], 1)
                if e == 7:
                    pe.wait_ge(s["b_xl"], u + 1)
                    for q in range(Q):
                        xs = slice(q * P, (q + 1) * P)
                        o = bkZ[:, q * E:(q + 1) * E]
                        mm(o, xh[up][:, xs], wrt_lo[:, :], True, False)
                        mm(o, xl[up][:, xs], wrt_hi[:, :], False, False)
                        i = mm(o, xh[up][:, xs], wrt_hi[:, :], False, True)
                    i.then_inc(s["b_lg"], 1)

            def b_gT(u, up):
                pe.wait_ge(s["b_g3"], 3 * u + 3)
                for q in range(Q):
                    i = pe.transpose(bkX[0:3 * PG, q * P:(q + 1) * P], g3[:, 3 * PG * q:3 * PG * (q + 1)], ident[:, :])
                i.then_inc(s["b_gT"], 1)

            def b_bias(u):
                pe.wait_ge(s["b_g3T"], u + 1)
                for q in range(Q):
                    i = mm(bkZ[:, q * P:(q + 1) * P], g3T[:, q * P:(q + 1) * P], bps[:, :])
                i.then_inc(s["b_bias"], 1)

            def b_fc(g, e, up, lead):
                if is_int(g) and g < EXP:
                    pe.wait_ge(s["split_lo"], fc(e) + 1)
                for j in range(J):
                    if not lead:
                        pe.wait_ge(s["b_gelu"], J * (g - 1) + j + 1)
                    js = slice(j * P, (j + 1) * P)
                    mm(bkF[j][:, :], w_lo(fc(e))[:, js], xh[up], True, False)
                    mm(bkF[j][:, :], w_hi(fc(e))[:, js], xl[up], False, False)
                    mm(bkF[j][:, :], w_hi(fc(e))[:, js], xh[up], False, True).then_inc(s["b_fc"], 1)

            def b_proj(g, e, par):
                if is_int(g) and g < EXP:
                    pe.wait_ge(s["split_lo"], proj(e) + 1)
                pe.wait_ge(s["b_lo"], J * (g + 1) + J)
                pe.wait_ge(s["b_comb"], Q * (g + 1))
                for q in range(Q):
                    o = bkP[par][:, q * P:(q + 1) * P]
                    qs = slice(q * P, (q + 1) * P)
                    for j in range(J):
                        js = slice(j * P, (j + 1) * P)
                        mm(o, hl[par][j][:, qs], w_hi(proj(e))[:, js], j == 0, False)
                        mm(o, hh[par][j][:, qs], w_lo(proj(e))[:, js], False, False)
                        i = mm(o, hh[par][j][:, qs], w_hi(proj(e))[:, js], False, j == J - 1)
                i.then_inc(s["b_proj"], 1)

            def b_tile(t, tp):
                last = is_int(t) and t + 1 == TILES
                for e in range(EXP):
                    g = EXP * t + e
                    if not last and e != 2:
                        b_piece(t + 1, e, 1 - tp)
                    if e == 0:
                        b_gT(t, tp)
                    if e + 1 < EXP:
                        b_fc(g + 1, e + 1, tp, False)
                    elif not last:
                        b_fc(g + 1, 0, 1 - tp, False)
                    if e == 0:
                        b_bias(t)
                    if not last and e == 2:
                        b_piece(t + 1, e, 1 - tp)
                    b_proj(g, e, (EXP * tp + e) % 2)

            pe.wait_ge(s["setup_ev"], 5)
            pe.wait_ge(s["decay_r"], 2)
            a_k(0)
            pe.wait_ge(s["wvrep_done"], N)
            a_vrep(0, 0, 0, True)
            a_vrep(0, 0, 1, True)
            a_r(0)
            a_g(0)
            pe.wait_ge(s["other_params_in"], N_OTHER_PARAMS)
            pe.transpose(bank[0][:, 0:C], woraw, ident[:, :]).then_inc(s["late_t"], 1)
            pe.transpose(bank[1][:, 0:NB - NB_MAA], prow_rest, ident[0:NB - NB_MAA, 0:NB - NB_MAA])\
              .then_inc(s["late_t"], 1)
            a_tile(0, 0, True, False)
            a_tile(1, 1, False, False)
            with pe.Fori(1, PAIRS - 1) as i:
                a_tile(2 * i, 0, False, False)
                a_tile(2 * i + 1, 1, False, False)
            a_tile(TILES - 2, 0, False, False)
            a_tile(TILES - 1, 1, False, True)
            pe.wait_ge(s["a_rk"], TILES)
            b_piece(0, 1, 0)
            a_sel(TILES - 1, N - 2)
            a_sel(TILES - 1, N - 1)
            pe.wait_ge(s["a_yu"], TILES)
            b_piece(0, 2, 0)
            a_yT(TILES - 1)
            b_piece(0, 6, 0)
            pe.wait_ge(s["a_y"], 2 * TILES)
            pe.wait_ge(s["late_lo"], 2)
            pe.wait_ge(s["g3_zero"], 1)
            b_piece(0, 7, 0)
            b_fc(0, 0, 0, True)
            b_tile(0, 0)
            b_tile(1, 1)
            with pe.Fori(1, PAIRS - 1) as i:
                b_tile(2 * i, 0)
                b_tile(2 * i + 1, 1)
            b_tile(TILES - 2, 0)
            b_tile(TILES - 1, 1)


_INS = ['L0_attn_x', 'L0_attn_time_maa_k', 'L0_attn_time_maa_v', 'L0_attn_time_maa_r', 'L0_attn_time_maa_g',
        'L0_attn_time_decay', 'L0_attn_time_faaaa', 'L0_attn_Wr', 'L0_attn_Wk', 'L0_attn_Wv', 'L0_attn_Wg',
        'L0_attn_Wo', 'L0_attn_ln_w', 'L0_attn_ln_b', 'L0_ffn_Wfc_s', 'L0_ffn_bfc_s', 'L0_ffn_Wproj_s',
        'L0_ffn_bproj_s', 'L0_ffn_Wr', 'L0_ffn_Wfc', 'L0_ffn_bfc', 'L0_ffn_Wproj', 'L0_ffn_bproj']
_OUT = (8, 1024, 128)


def kernel(**inputs):
    import numpy as _np
    import concourse.bacc as _bacc
    from concourse.bass_utils import run_bass_kernel_spmd as _run

    nc = _bacc.Bacc("TRN2", target_bir_lowering=False, num_devices=1)
    arrays, args = {}, []
    for name in _INS:
        a = _np.ascontiguousarray(inputs[name])
        arrays[f"in_{name}"] = a
        args.append(nc.dram_tensor(f"in_{name}", a.shape, mybir.dt.from_np(a.dtype), kind="ExternalInput").ap())
    args.append(nc.dram_tensor("out_0", _OUT, F32, kind="ExternalOutput").ap())
    build(nc, *args)
    r = _run(nc, [arrays], core_ids=[0])
    return r.results[0]["out_0"]
```
